# Optimizing a Trainium2 kernel written in Bass

```python
import numpy as np
import jax
import jax.numpy as jnp

def _softmax(x, axis=-1):
    return jax.nn.softmax(x, axis=axis)

def _gelu(x):
    return jax.nn.gelu(x, approximate=True)

def _silu(x):
    return jax.nn.silu(x)

def _sigmoid(x):
    return jax.nn.sigmoid(x)

def _layernorm(x, axis=-1, eps=1e-05):
    m = jnp.mean(x, axis=axis, keepdims=True)
    v = jnp.var(x, axis=axis, keepdims=True)
    return (x - m) / jnp.sqrt(v + eps)

def _scatter_add(tgt, idx, src, axis=0):
    return tgt.at[idx].add(src)

def _segment_sum(src, seg, n):
    return jax.ops.segment_sum(src, seg, n)
kernel_name = 'mk_adj_seq_d4_adj_r2_19ef88'

def setup_inputs(seed: int=0):
    np.random.seed(seed)
    _w = jnp.asarray

    def _rec_inputs():
        import jax
        import jax.numpy as jnp
        _gk = jax.random.key(seed)
        x = -0.0002928 + 1 * jax.random.normal(jax.random.fold_in(_gk, 1), (128, 128, 256), jnp.float32)
        _a = jax.random.bernoulli(jax.random.fold_in(_gk, 2), 0.0625, (128, 128, 128))
        _a = jnp.logical_or(_a, jnp.swapaxes(_a, -1, -2))
        _a = jnp.logical_or(_a, jnp.eye(128, dtype=bool))
        _af = _a.astype(jnp.float32)
        _af = _af / jnp.maximum(_af.sum(-1, keepdims=True), 1.0)
        adj = _af
        return (x, adj)
    x, adj = _rec_inputs()

    def _L0_gnn_setup():
        import jax, jax.numpy as jnp
        import numpy as np
        B, N, D, H = (8, 512, 256, 8)
        DK = D // H
        LN_EPS = 1e-05
        ADJ_MIN = 1e-08

        def _layer_norm(x, gamma, beta):
            mu = jnp.mean(x, axis=-1, keepdims=True)
            var = jnp.mean(jnp.square(x - mu), axis=-1, keepdims=True)
            return (x - mu) * jax.lax.rsqrt(var + LN_EPS) * gamma + beta
        key = jax.random.key(seed)
        ks = jax.random.split(key, 12)
        x = jax.random.normal(ks[0], (B, N, D), dtype=jnp.float32)
        adj = jax.random.uniform(ks[1], (B, N, N), dtype=jnp.float32)
        adj = adj / jnp.sum(adj, axis=-1, keepdims=True)
        s = 1.0 / np.sqrt(D)
        Wq = jax.random.normal(ks[2], (D, D), dtype=jnp.float32) * s
        bq = jnp.zeros((D,), dtype=jnp.float32)
        Wk = jax.random.normal(ks[3], (D, D), dtype=jnp.float32) * s
        bk = jnp.zeros((D,), dtype=jnp.float32)
        Wv = jax.random.normal(ks[4], (D, D), dtype=jnp.float32) * s
        bv = jnp.zeros((D,), dtype=jnp.float32)
        Wo = jax.random.normal(ks[5], (D, D), dtype=jnp.float32) * s
        bo = jnp.zeros((D,), dtype=jnp.float32)
        gamma = jnp.ones((D,), dtype=jnp.float32)
        beta = jnp.zeros((D,), dtype=jnp.float32)
        return {'x': x, 'adj': adj, 'Wq': Wq, 'bq': bq, 'Wk': Wk, 'bk': bk, 'Wv': Wv, 'bv': bv, 'Wo': Wo, 'bo': bo, 'gamma': gamma, 'beta': beta}
    _L0_gnn_all = _L0_gnn_setup()
    _L0_gnn_in = {k: v for k, v in _L0_gnn_all.items() if k in ('Wq', 'bq', 'Wk', 'bk', 'Wv', 'bv', 'Wo', 'bo', 'gamma', 'beta')}
    del _L0_gnn_all

    def _L1_gnn_setup():
        import jax, jax.numpy as jnp
        import numpy as np
        BS, N, H = (8, 1024, 256)
        NEG_INF = -1000000000.0
        LEAKY_SLOPE = 0.01
        key = jax.random.key(seed)
        ks = jax.random.split(key, 8)
        feats = jax.random.normal(ks[0], (BS, N, H), dtype=jnp.float32)
        adj = jax.random.randint(ks[1], (BS, N, N), 0, 2).astype(jnp.float32)
        adj = jnp.maximum(adj, jnp.eye(N, dtype=jnp.float32)[None])
        s = 1.0 / np.sqrt(H)
        return {'feats': feats, 'adj_mat': adj, 'fc_w': jax.random.normal(ks[2], (H, H), dtype=jnp.float32) * s, 'fc_b': jax.random.normal(ks[3], (H,), dtype=jnp.float32) * s, 'q_w': jax.random.normal(ks[4], (1, H), dtype=jnp.float32) * s, 'q_b': jax.random.normal(ks[5], (1,), dtype=jnp.float32) * s, 'k_w': jax.random.normal(ks[6], (1, H), dtype=jnp.float32) * s, 'k_b': jax.random.normal(ks[7], (1,), dtype=jnp.float32) * s}
    _L1_gnn_all = _L1_gnn_setup()
    _L1_gnn_in = {k: v for k, v in _L1_gnn_all.items() if k in ('fc_w', 'fc_b', 'q_w', 'q_b', 'k_w', 'k_b')}
    del _L1_gnn_all

    def _L2_gnn_setup():
        import jax, jax.numpy as jnp
        import numpy as np
        NUM_HEADS = 8
        EPS = 1e-09
        key = jax.random.key(seed)
        ks = jax.random.split(key, 8)
        B, N, D = (2, 1024, 256)
        s = 1.0 / np.sqrt(D)
        x = jax.random.normal(ks[0], (B, N, D), dtype=jnp.float32)
        adjacency = jax.random.uniform(ks[1], (B, N, N), dtype=jnp.float32)
        W_q = jax.random.normal(ks[2], (D, D), dtype=jnp.float32) * s
        W_k = jax.random.normal(ks[3], (D, D), dtype=jnp.float32) * s
        W_v = jax.random.normal(ks[4], (D, D), dtype=jnp.float32) * s
        b_q = jnp.zeros((D,), jnp.float32)
        b_k = jnp.zeros((D,), jnp.float32)
        b_v = jnp.zeros((D,), jnp.float32)
        w_g = jax.random.normal(ks[5], (2 * D,), dtype=jnp.float32) * (1.0 / np.sqrt(2 * D))
        b_g = jnp.zeros((), jnp.float32)
        return {'x': x, 'adjacency': adjacency, 'W_q': W_q, 'b_q': b_q, 'W_k': W_k, 'b_k': b_k, 'W_v': W_v, 'b_v': b_v, 'w_g': w_g, 'b_g': b_g}
    _L2_gnn_all = _L2_gnn_setup()
    _L2_gnn_in = {k: v for k, v in _L2_gnn_all.items() if k in ('W_q', 'b_q', 'W_k', 'b_k', 'W_v', 'b_v', 'w_g', 'b_g')}
    del _L2_gnn_all

    def _L3_gnn_setup():
        import jax, jax.numpy as jnp
        import numpy as np
        NUM_HID = 256
        BS, N = (8, 1024)
        NEG_BIG = -1000000000.0
        LEAKY_SLOPE = 0.01
        key = jax.random.key(seed)
        k_feats, k_adj, k_w, k_wq, k_wk = jax.random.split(key, 5)
        feats = jax.random.normal(k_feats, (BS, N, NUM_HID), dtype=jnp.float32)
        adj = (jax.random.uniform(k_adj, (BS, N, N)) < 0.05).astype(jnp.float32)
        eye = jnp.eye(N, dtype=jnp.float32)[None]
        adj_mat = jnp.maximum(adj, eye)
        s = 1.0 / np.sqrt(NUM_HID)
        W_fc = jax.random.uniform(k_w, (NUM_HID, NUM_HID), minval=-s, maxval=s, dtype=jnp.float32)
        b_fc = jnp.zeros((NUM_HID,), dtype=jnp.float32)
        w_q = jax.random.uniform(k_wq, (NUM_HID, 1), minval=-s, maxval=s, dtype=jnp.float32)
        b_q = jnp.zeros((1,), dtype=jnp.float32)
        w_k = jax.random.uniform(k_wk, (NUM_HID, 1), minval=-s, maxval=s, dtype=jnp.float32)
        b_k = jnp.zeros((1,), dtype=jnp.float32)
        return {'feats': feats, 'adj_mat': adj_mat, 'W_fc': W_fc, 'b_fc': b_fc, 'w_q': w_q, 'b_q': b_q, 'w_k': w_k, 'b_k': b_k}
    _L3_gnn_all = _L3_gnn_setup()
    _L3_gnn_in = {k: v for k, v in _L3_gnn_all.items() if k in ('W_fc', 'b_fc', 'w_q', 'b_q', 'w_k', 'b_k')}
    del _L3_gnn_all
    return {'x': x, 'adj': adj, 'L0_gnn_Wq': _L0_gnn_in['Wq'], 'L0_gnn_bq': _L0_gnn_in['bq'], 'L0_gnn_Wk': _L0_gnn_in['Wk'], 'L0_gnn_bk': _L0_gnn_in['bk'], 'L0_gnn_Wv': _L0_gnn_in['Wv'], 'L0_gnn_bv': _L0_gnn_in['bv'], 'L0_gnn_Wo': _L0_gnn_in['Wo'], 'L0_gnn_bo': _L0_gnn_in['bo'], 'L0_gnn_gamma': _L0_gnn_in['gamma'], 'L0_gnn_beta': _L0_gnn_in['beta'], 'L1_gnn_fc_w': _L1_gnn_in['fc_w'], 'L1_gnn_fc_b': _L1_gnn_in['fc_b'], 'L1_gnn_q_w': _L1_gnn_in['q_w'], 'L1_gnn_q_b': _L1_gnn_in['q_b'], 'L1_gnn_k_w': _L1_gnn_in['k_w'], 'L1_gnn_k_b': _L1_gnn_in['k_b'], 'L2_gnn_W_q': _L2_gnn_in['W_q'], 'L2_gnn_b_q': _L2_gnn_in['b_q'], 'L2_gnn_W_k': _L2_gnn_in['W_k'], 'L2_gnn_b_k': _L2_gnn_in['b_k'], 'L2_gnn_W_v': _L2_gnn_in['W_v'], 'L2_gnn_b_v': _L2_gnn_in['b_v'], 'L2_gnn_w_g': _L2_gnn_in['w_g'], 'L2_gnn_b_g': _L2_gnn_in['b_g'], 'L3_gnn_W_fc': _L3_gnn_in['W_fc'], 'L3_gnn_b_fc': _L3_gnn_in['b_fc'], 'L3_gnn_w_q': _L3_gnn_in['w_q'], 'L3_gnn_b_q': _L3_gnn_in['b_q'], 'L3_gnn_w_k': _L3_gnn_in['w_k'], 'L3_gnn_b_k': _L3_gnn_in['b_k']}

def reference(x, adj, L0_gnn_Wq, L0_gnn_bq, L0_gnn_Wk, L0_gnn_bk, L0_gnn_Wv, L0_gnn_bv, L0_gnn_Wo, L0_gnn_bo, L0_gnn_gamma, L0_gnn_beta, L1_gnn_fc_w, L1_gnn_fc_b, L1_gnn_q_w, L1_gnn_q_b, L1_gnn_k_w, L1_gnn_k_b, L2_gnn_W_q, L2_gnn_b_q, L2_gnn_W_k, L2_gnn_b_k, L2_gnn_W_v, L2_gnn_b_v, L2_gnn_w_g, L2_gnn_b_g, L3_gnn_W_fc, L3_gnn_b_fc, L3_gnn_w_q, L3_gnn_b_q, L3_gnn_w_k, L3_gnn_b_k):
    import jax
    import jax.numpy as jnp

    def _L0_gnn_ref(x, adj, Wq, bq, Wk, bk, Wv, bv, Wo, bo, gamma, beta):
        import jax, jax.numpy as jnp
        import numpy as np
        B, N, D, H = (8, 512, 256, 8)
        DK = D // H
        LN_EPS = 1e-05
        ADJ_MIN = 1e-08

        def _layer_norm(x, gamma, beta):
            mu = jnp.mean(x, axis=-1, keepdims=True)
            var = jnp.mean(jnp.square(x - mu), axis=-1, keepdims=True)
            return (x - mu) * jax.lax.rsqrt(var + LN_EPS) * gamma + beta
        b, n, d = x.shape
        q = (x @ Wq.T + bq).reshape(b, n, H, DK).transpose(0, 2, 1, 3)
        k = (x @ Wk.T + bk).reshape(b, n, H, DK).transpose(0, 2, 1, 3)
        v = (x @ Wv.T + bv).reshape(b, n, H, DK).transpose(0, 2, 1, 3)
        logits = jnp.einsum('bhqd,bhkd->bhqk', q, k) / np.sqrt(DK)
        logits = logits + jnp.log(jnp.clip(adj, ADJ_MIN, None))[:, None, :, :]
        attn = jax.nn.softmax(logits, axis=-1)
        out = jnp.einsum('bhqk,bhkd->bhqd', attn, v)
        out = out.transpose(0, 2, 1, 3).reshape(b, n, d)
        out = out @ Wo.T + bo
        return _layer_norm(x + out, gamma, beta)

    def _L1_gnn_ref(feats, adj_mat, fc_w, fc_b, q_w, q_b, k_w, k_b):
        import jax, jax.numpy as jnp
        import numpy as np
        BS, N, H = (8, 1024, 256)
        NEG_INF = -1000000000.0
        LEAKY_SLOPE = 0.01
        feat_proj = jnp.einsum('bnh,oh->bno', feats, fc_w) + fc_b
        q = jnp.einsum('bnh,oh->bno', feat_proj, q_w) + q_b
        k = jnp.einsum('bnh,oh->bno', feat_proj, k_w) + k_b
        logits = q + jnp.swapaxes(k, 2, 1)
        masked = logits + (1.0 - adj_mat) * NEG_INF
        masked = jnp.where(masked >= 0, masked, LEAKY_SLOPE * masked)
        atten = jax.nn.softmax(masked, axis=-1)
        out = jnp.einsum('bnm,bmh->bnh', atten, feat_proj)
        return out + feats

    def _L2_gnn_ref(x, adjacency, W_q, b_q, W_k, b_k, W_v, b_v, w_g, b_g):
        import jax, jax.numpy as jnp
        import numpy as np
        NUM_HEADS = 8
        EPS = 1e-09
        B, N, D = x.shape
        H = NUM_HEADS
        hd = D // H
        Q = (x @ W_q + b_q).reshape(B, N, H, hd)
        K = (x @ W_k + b_k).reshape(B, N, H, hd)
        V = (x @ W_v + b_v).reshape(B, N, H, hd)
        scores = jnp.einsum('bihd,bjhd->bhij', Q, K) / jnp.sqrt(jnp.float32(hd))
        a = x @ w_g[:D]
        c = x @ w_g[D:]
        soul_bias = a[:, :, None] + c[:, None, :] + b_g
        scores = scores + (soul_bias + jnp.log(adjacency + EPS))[:, None, :, :]
        attn = jax.nn.softmax(scores, axis=-1)
        out = jnp.einsum('bhij,bjhd->bihd', attn, V).reshape(B, N, D)
        return out + x

    def _L3_gnn_ref(feats, adj_mat, W_fc, b_fc, w_q, b_q, w_k, b_k):
        import jax, jax.numpy as jnp
        import numpy as np
        NUM_HID = 256
        BS, N = (8, 1024)
        NEG_BIG = -1000000000.0
        LEAKY_SLOPE = 0.01
        feat_proj = jnp.einsum('bnd,de->bne', feats, W_fc) + b_fc
        q = jnp.einsum('bnd,do->bno', feat_proj, w_q) + b_q
        k = jnp.einsum('bnd,do->bno', feat_proj, w_k) + b_k
        logits = q + jnp.swapaxes(k, 2, 1)
        masked = logits + (1.0 - adj_mat) * NEG_BIG
        masked = jnp.where(masked >= 0, masked, LEAKY_SLOPE * masked)
        atten = jax.nn.softmax(masked, axis=-1)
        out = jnp.einsum('bnm,bmd->bnd', atten, feat_proj)
        return out + feats
    x = _L0_gnn_ref(x, adj, L0_gnn_Wq, L0_gnn_bq, L0_gnn_Wk, L0_gnn_bk, L0_gnn_Wv, L0_gnn_bv, L0_gnn_Wo, L0_gnn_bo, L0_gnn_gamma, L0_gnn_beta)
    x = _L1_gnn_ref(x, adj, L1_gnn_fc_w, L1_gnn_fc_b, L1_gnn_q_w, L1_gnn_q_b, L1_gnn_k_w, L1_gnn_k_b)
    x = _L2_gnn_ref(x, adj, L2_gnn_W_q, L2_gnn_b_q, L2_gnn_W_k, L2_gnn_b_k, L2_gnn_W_v, L2_gnn_b_v, L2_gnn_w_g, L2_gnn_b_g)
    x = _L3_gnn_ref(x, adj, L3_gnn_W_fc, L3_gnn_b_fc, L3_gnn_w_q, L3_gnn_b_q, L3_gnn_w_k, L3_gnn_b_k)
    return x

_drawn_inputs = setup_inputs


def setup_inputs(seed=0):
    import zlib

    import numpy as np

    out = dict(_drawn_inputs(seed))
    spreads = {'L0_gnn_bq': (0.0, 0.1),
     'L0_gnn_bk': (0.0, 2.0),
     'L0_gnn_bv': (0.0, 0.1),
     'L0_gnn_bo': (0.0, 0.1),
     'L0_gnn_gamma': (1.0, 0.2),
     'L0_gnn_beta': (0.0, 0.1),
     'L2_gnn_b_q': (0.0, 0.315),
     'L2_gnn_b_k': (0.0, 2.0),
     'L2_gnn_b_v': (0.0, 0.1),
     'L3_gnn_b_fc': (0.0, 0.1)}
    factors = {'L3_gnn_w_q': 18.701, 'L3_gnn_w_k': 10.424}
    for name, (base, spread) in spreads.items():
        noise = np.random.default_rng([zlib.crc32(name.encode()), seed]).standard_normal(out[name].shape)
        drawn = base * np.exp(spread * noise) if base else spread * noise
        out[name] = jnp.asarray(drawn.astype(out[name].dtype))
    for name, factor in factors.items():
        out[name] = (out[name] * factor).astype(out[name].dtype)
    return out
```

```python
import concourse.bass as bass
from concourse import mybir
from contextlib import ExitStack

F32 = mybir.dt.float32
F32R = mybir.dt.float32r
ALU = mybir.AluOpType
ACT = mybir.ActivationFunctionType
AX = mybir.AxisListType

P = 128
GROUP = 4
HEADS, HEAD_DIM = 8, 32
HALF = 4
UNITS = GROUP * 2
KT = 2
BANKS = 8
ADJ_MIN, ADJ_EPS, LN_EPS, PENALTY, SLOPE = 1e-8, 1e-9, 1e-5, 1e9, 0.01
SCALE = 1.0 / float(HEAD_DIM) ** 0.5

OFFSET = {"A": 0, "B": 1}
TURN, USE, FINISH, SPLIT = 2, 3, 4, 5
SCORE_BANK = {"A": 0, "B": 2}
HEADS_BANK = {"A": 4, "B": 6}


def attention_steps(streams):
    for position in range(2 * (UNITS - 1) + 1 + SPLIT + 1):
        for stage, lag in (("scores", 0), ("weigh", 1), ("turn", TURN), ("use", USE),
                           ("finish", FINISH), ("split", SPLIT)):
            for stream in streams:
                unit, odd = divmod(position - lag - OFFSET[stream], 2)
                if not odd and 0 <= unit < UNITS:
                    yield stage, stream, unit


class Body:

    def __init__(self, has_in, has_mid, has_tail):
        self.has_in, self.has_mid, self.has_tail = has_in, has_mid, has_tail
        self.streams = ("A",) * has_mid + ("B",) * has_tail

    def tensor_steps(self):
        steps = [s for s in attention_steps(self.streams) if s[0] in ("scores", "turn", "use")]
        present = {"in": self.has_in, "mid": self.has_mid, "tail": self.has_tail}
        return steps + [step for when, *step in BETWEEN if present[when]]

    def fills(self):
        out = []
        for step, stream, n in self.tensor_steps():
            if step in ("scores", "turn"):
                out.append(((step, stream, n), SCORE_BANK[stream] + n % 2))
            elif step == "use":
                if n % 2 == 0:
                    out.append((("heads", stream, n // 2), HEADS_BANK[stream] + n // 2 % 2))
            else:
                out.append(((step, stream, n), BETWEEN_BANK[step, stream, n]))
        return out


def between():
    tiles, graphs = range(KT), range(GROUP)
    plan = [("mid", "out_proj", "0", graphs), ("tail", "turn_back", "2", graphs),
            ("tail", "turn_x", "3", tiles), ("tail", "fc", "3", graphs), ("tail", "spread_k", "3", [0]),
            ("mid", "turn_x", "1", tiles), ("mid", "fc", "1", graphs), ("mid", "spread_k", "1", [0]),
            ("in", "turn_x", "0", tiles), ("in", "k", "0", tiles), ("in", "q", "0", tiles),
            ("tail", "turn_p", "3", [0]), ("tail", "mix", "3", graphs),
            ("mid", "turn_p", "1", [0]), ("mid", "mix", "1", graphs),
            ("in", "v", "0", graphs),
            ("mid", "turn_x", "2", tiles), ("mid", "k", "2", tiles), ("mid", "q", "2", tiles),
            ("mid", "v", "2", graphs), ("mid", "turn_rows", "2", range(2))]
    return [(when, step, layer, n) for when, step, layer, ns in plan for n in ns]


BETWEEN = between()
BETWEEN_BANK = {step[1:]: i % BANKS for i, step in enumerate(BETWEEN)}


class Banks:

    def __init__(self, fills, start, held):
        self.place, self.start, self.before = {}, start, {}
        self.count = [0] * BANKS
        held = {b: (key, back) for b, (key, back) in held.items()}
        for key, bank in fills:
            self.place[key] = (bank, self.count[bank])
            self.before[key] = held.get(bank)
            self.count[bank] += 1
            held[bank] = (key, 0)
        self.held = {b: (key, back + 1) for b, (key, back) in held.items()}

    def bank(self, *key):
        return self.place[key][0]

    def after(self, *key):
        bank, n = self.place[key]
        return self.start[bank] + n + 1


def build_kernel(nc, ins, out):
    GRAPHS, NODES, DIM = ins["x"].shape
    assert NODES == P and DIM == KT * P and GRAPHS % GROUP == 0
    GROUPS = GRAPHS // GROUP
    WIDE = DIM + 2
    x_dram = ins["x"].rearrange("(t g) n d -> t n g d", g=GROUP)
    adj_dram = ins["adj"].rearrange("(t g) n m -> t n g m", g=GROUP)
    out_dram = out.rearrange("(t g) n d -> t n g d", g=GROUP)

    with ExitStack() as ctx:
        def sb(name, shape, dt=F32):
            return ctx.enter_context(nc.sbuf_tensor(name, shape, dt))

        def sem(name):
            return ctx.enter_context(nc.semaphore(name))

        ctx.enter_context(nc.allow_non_contiguous_dma(reason="weight columns, once"))

        bank = [ctx.enter_context(nc.psum_tensor(f"bank{b}", [P, 512], F32)) for b in range(BANKS)]
        filled = [sem(f"filled{b}") for b in range(BANKS)]

        x_in = sb("x_in", [P, GROUP, DIM])
        x_1 = sb("x_1", [P, GROUP, DIM])
        x_2 = sb("x_2", [P, GROUP, DIM])
        x_3 = sb("x_3", [P, GROUP, DIM])
        x_out = sb("x_out", [P, GROUP, DIM])
        resid = {"0": x_in, "1": x_1, "2": x_2, "3": x_3}
        adj = sb("adj", [P, GROUP, P])
        adj_0 = sb("adj_0", [P, GROUP, P])
        adj_2 = sb("adj_2", [P, GROUP, P])
        penalty = {n: sb(f"penalty_{n}", [P, GROUP, P]) for n in "13"}
        weight_of = {"A": adj_0, "B": adj_2}

        xt_hi = {s: sb(f"xt_hi_{s}", [P, KT, GROUP * P], F32R) for s in "AB"}
        xt_lo = {s: sb(f"xt_lo_{s}", [P, KT, GROUP * P], F32R) for s in "AB"}
        xt_of = {"0": "A", "1": "B", "2": "B", "3": "B"}

        qt = {s: sb(f"qt_{s}", [P, KT, GROUP * P]) for s in "AB"}
        kt = {s: sb(f"kt_{s}", [P, KT, GROUP * P]) for s in "AB"}
        kt_diag = {s: sb(f"kt_diag_{s}", [P, KT, GROUP, HALF, P]) for s in "AB"}
        v = {"A": sb("v_A", [P, GROUP, DIM]), "B": sb("v_B", [P, GROUP, WIDE])}
        scratch = sb("scratch", [P, 6, 2, 512])
        e = {s: scratch[:, 3 * n + 0] for n, s in enumerate("AB")}
        pr = {s: scratch[:, 3 * n + 1] for n, s in enumerate("AB")}
        pt = {s: scratch[:, 3 * n + 2] for n, s in enumerate("AB")}
        neg_max = {s: sb(f"neg_max_{s}", [P, 2, HALF]) for s in "AB"}
        den = {s: sb(f"den_{s}", [P, 2, HALF]) for s in "AB"}
        inv_den = {s: sb(f"inv_den_{s}", [P, GROUP, HEADS]) for s in "AB"}
        inv_wide = sb("inv_wide", [P, 2, P])
        inv_den_t = sb("inv_den_t", [P, 2, DIM])
        ot = {"A": sb("ot_A", [P, 2, DIM]), "B": sb("ot_B", [P, GROUP, DIM])}
        ot_hi = sb("ot_hi", [P, GROUP, DIM], F32R)
        ot_lo = sb("ot_lo", [P, GROUP, DIM], F32R)
        ac_sum = sb("ac_sum", [P, GROUP, 2])
        ac_cols = sb("ac_cols", [P, GROUP, 8], F32R)
        ac_rows = [sb(f"ac_rows{n}", [4, GROUP * P], F32R) for n in range(2)]

        fp = {n: sb(f"fp_{n}", [P, GROUP, WIDE]) for n in "13"}
        logits = {n: sb(f"logits_{n}", [P, GROUP, P]) for n in "13"}
        fpt = {n: sb(f"pt_{n}", [P, GROUP, P]) for n in "13"}
        f_neg_max = {n: sb(f"f_neg_max_{n}", [P, GROUP]) for n in "13"}
        f_den = {n: sb(f"f_den_{n}", [P, GROUP]) for n in "13"}
        f_inv = {n: sb(f"f_inv_{n}", [P, GROUP]) for n in "13"}

        stats = sb("stats", [P, GROUP, 6])
        moments = sb("moments", [P, GROUP, 2])
        rstd = sb("rstd", [P, GROUP])
        one, big, adj_eps, ln_eps, minus_half = (
            sb(name, [P, 1]) for name in ("one", "big", "adj_eps", "ln_eps", "minus_half"))

        ident = sb("ident", [P, P])
        w_hi = {n: sb(f"w_hi_{n}", [P, KT, WIDE], F32R) for n in ("q0", "k0", "v0", "o0", "f1", "q2", "k2", "v2", "f3")}
        w_lo = {n: sb(f"w_lo_{n}", [P, KT, WIDE], F32R) for n in w_hi}
        SOURCE = {"q0": "L0_gnn_Wq", "k0": "L0_gnn_Wk", "v0": "L0_gnn_Wv", "o0": "L0_gnn_Wo", "f1": "L1_gnn_fc_w",
                  "q2": "L2_gnn_W_q", "k2": "L2_gnn_W_k", "v2": "L2_gnn_W_v", "f3": "L3_gnn_W_fc"}
        RAW_ORDER = list(SOURCE)
        flat = scratch[:, :, :, :].rearrange("p a b c -> p (a b c)")
        raw = {n: flat[:, i * 512:(i + 1) * 512].rearrange("p (k e) -> p k e", k=KT) for i, n in enumerate(RAW_ORDER)}
        w3_t = flat[:, 9 * 512:10 * 512].rearrange("p (k e) -> p k e", k=KT)
        bias_cols = {n: sb(f"bias_{n}", [P, KT]) for n in ("q0", "k0", "q2", "k2")}
        bv_col = sb("bv_col", [P, KT])
        fc_bias_col = {n: sb(f"fc_bias_col_{n}", [P, KT]) for n in "13"}
        qk_w = {n: sb(f"qk_w_{n}", [P, KT, 2]) for n in "13"}
        qk_b = {n: sb(f"qk_b_{n}", [P, 2]) for n in "13"}
        soul_w = sb("soul_w", [P, KT, 2])
        soul_b = sb("soul_b", [P, 2])
        rows = {n: sb(f"row_{n}", [P, DIM]) for n in ("gamma", "beta", "b1", "b2", "b3")}
        out_bias = sb("out_bias", [P, DIM])

        CONSTANTS = 10

        x_landed, adj_landed, stored = sem("x_landed"), sem("adj_landed"), sem("stored")
        kd_landed = {s: sem(f"kd_landed_{s}") for s in "AB"}
        raw_landed, small_landed = sem("raw_landed"), sem("small_landed")
        const_ready = sem("const_ready")
        setup_act, setup_dve = sem("setup_act"), sem("setup_dve")
        xt_hi_ready = {n: sem(f"xt_hi_ready_{n}") for n in "0123"}
        xt_ready = {n: sem(f"xt_ready_{n}") for n in "0123"}
        qt_ready = {s: sem(f"qt_ready_{s}") for s in "AB"}
        kt_ready = {s: sem(f"kt_ready_{s}") for s in "AB"}
        v_ready = {s: sem(f"v_ready_{s}") for s in "AB"}
        maxed = {s: sem(f"maxed_{s}") for s in "AB"}
        exped = {s: sem(f"exped_{s}") for s in "AB"}
        weighed = {s: sem(f"weighed_{s}") for s in "AB"}
        inverted = {s: sem(f"inverted_{s}") for s in "AB"}
        pt_ready = {s: sem(f"pt_ready_{s}") for s in "AB"}
        inv_spread = sem("inv_spread")
        inv_t_ready = sem("inv_t_ready")
        ot_ready = {s: sem(f"ot_ready_{s}") for s in "AB"}
        ot_hi_ready, ot_lo_ready = sem("ot_hi_ready"), sem("ot_lo_ready")
        summed, stats_ready, moments_ready = sem("summed"), sem("stats_ready"), sem("moments_ready")
        var_ready, rstd_ready = sem("var_ready"), sem("rstd_ready")
        centred, x1_ready = sem("centred"), sem("x1_ready")
        x2_ready, x3_scaled = sem("x2_ready"), sem("x3_scaled")
        x3_ready = sem("x3_ready")
        x_biased = {n: sem(f"x_biased_{n}") for n in "0123"}
        out_ready = sem("out_ready")
        fp_ready = {n: sem(f"fp_ready_{n}") for n in "13"}
        qk_ready = {n: sem(f"qk_ready_{n}") for n in "13"}
        masked = {n: sem(f"masked_{n}") for n in "13"}
        leaked = {n: sem(f"leaked_{n}") for n in "13"}
        f_maxed = {n: sem(f"f_maxed_{n}") for n in "13"}
        f_exped = {n: sem(f"f_exped_{n}") for n in "13"}
        f_inverted = {n: sem(f"f_inverted_{n}") for n in "13"}
        fpt_ready = {n: sem(f"fpt_ready_{n}") for n in "13"}
        adj0_ready, adj2_ready = sem("adj0_ready"), sem("adj2_ready")
        one_minus = {n: sem(f"one_minus_{n}") for n in "13"}
        penalty_ready = {n: sem(f"penalty_ready_{n}") for n in "13"}
        ac_summed, ac_hi_ready, ac_ready, ac_rows_ready = (
            sem("ac_summed"), sem("ac_hi_ready"), sem("ac_ready"), sem("ac_rows_ready"))

        def column(name):
            return ins[name].rearrange("(k p) -> p k", p=P)

        def row(name):
            return ins[name].partition_broadcast(P)

        small = [(bias_cols["q0"][:, :], column("L0_gnn_bq")), (bias_cols["k0"][:, :], column("L0_gnn_bk")),
                 (bias_cols["q2"][:, :], column("L2_gnn_b_q")), (bias_cols["k2"][:, :], column("L2_gnn_b_k")),
                 (bv_col[:, :], column("L0_gnn_bv")),
                 (fc_bias_col["1"][:, :], column("L1_gnn_fc_b")), (fc_bias_col["3"][:, :], column("L3_gnn_b_fc")),
                 (qk_w["1"][:, :, 0], ins["L1_gnn_q_w"].rearrange("a (k p) -> p (a k)", p=P)),
                 (qk_w["1"][:, :, 1], ins["L1_gnn_k_w"].rearrange("a (k p) -> p (a k)", p=P)),
                 (qk_w["3"][:, :, 0], ins["L3_gnn_w_q"].rearrange("(k p) a -> p (k a)", p=P)),
                 (qk_w["3"][:, :, 1], ins["L3_gnn_w_k"].rearrange("(k p) a -> p (k a)", p=P)),
                 (qk_b["1"][:, 0:1], row("L1_gnn_q_b")), (qk_b["1"][:, 1:2], row("L1_gnn_k_b")),
                 (qk_b["3"][:, 0:1], row("L3_gnn_b_q")), (qk_b["3"][:, 1:2], row("L3_gnn_b_k")),
                 (soul_w[:, :, 0], ins["L2_gnn_w_g"].rearrange("(c k p) -> c p k", p=P, k=KT)[0]),
                 (soul_w[:, :, 1], ins["L2_gnn_w_g"].rearrange("(c k p) -> c p k", p=P, k=KT)[1]),
                 (soul_b[:, 0:1], ins["L2_gnn_b_g"].partition_broadcast(P)),
                 (out_bias[:, :], row("L0_gnn_bo")), (rows["gamma"][:, :], row("L0_gnn_gamma")),
                 (rows["beta"][:, :], row("L0_gnn_beta")), (rows["b1"][:, :], row("L1_gnn_fc_b")),
                 (rows["b2"][:, :], row("L2_gnn_b_v")), (rows["b3"][:, :], row("L3_gnn_b_fc"))]
        SMALL_DONE = 16 * len(small)

        TURNED, DIRECT = ("q0", "k0", "v0", "o0", "f1"), ("q2", "k2", "v2", "f3")
        both = range(KT)
        ACT_STEPS = ([("hi", n, k) for n in TURNED for k in both] + [("w3_t", "", k) for k in both]
                     + [("hi", n, "all") for n in DIRECT] + [("hi", "soul", "all")]
                     + [("hi", "qk" + n, k) for n in "13" for k in both])
        DVE_STEPS = ([("lo", n, k) for n in TURNED for k in both] + [("lo", n, "all") for n in DIRECT]
                     + [("lo", "soul", "all")] + [("lo", "qk" + n, k) for n in "13" for k in both]
                     + [("zero", "", ""), ("scale", "q0", ""), ("scale", "q2", ""), ("scale", "soul_b", ""),
                        ("sum", "1", ""), ("neg", "1", ""), ("sum", "3", ""), ("neg", "3", ""), ("out_bias", "", "")])
        act_step = {key: i + 1 for i, key in enumerate(ACT_STEPS)}
        dve_step = {key: i + 1 for i, key in enumerate(DVE_STEPS)}
        SETUP_DONE = len(DVE_STEPS)

        setup_fills = []
        for i, key in enumerate(["t_q0", "t_k0", "t_v0", "t_o0", "t_f1", "t_f3", "qk1", "qk3", "c1", "c3", "out_bias"]):
            n_k = KT if key[:2] in ("t_", "qk") else 1
            setup_fills += [((key, k), (2 * i + k) % BANKS) for k in range(n_k)]
        setup = Banks(setup_fills, [0] * BANKS, {})

        entry, first, steady = Body(True, False, False), Body(True, True, False), Body(True, True, True)
        last, drain = Body(False, True, True), Body(False, False, True)

        def following(body, banks, turns=1):
            start = [n + turns * c for n, c in zip(banks.start, banks.count)]
            return Banks(body.fills(), start, banks.held)

        SETUP = (("setup", "", 0), 0)
        setup.held = {b: SETUP for b in range(BANKS)}
        in_entry = following(entry, setup)
        in_first = following(first, in_entry)
        in_steady = following(steady, in_first)
        in_last = following(last, in_steady, GROUPS - 2)
        in_drain = following(drain, in_last)
        assert in_steady.held == in_first.held

        def run(eng, task):
            task(entry, -1, in_entry)
            task(first, 0, in_first)
            with eng.Fori(1, GROUPS - 1) as t:
                start = [in_steady.start[b] + (t - 1) * in_steady.count[b] for b in range(BANKS)]
                task(steady, t, Banks(steady.fills(), start, in_first.held))
            task(last, GROUPS - 1, in_last)
            task(drain, GROUPS, in_drain)

        LAYER_GROUP = {"0": 1, "1": 0, "2": 0, "3": -1}

        def group_of(name, where, t):
            if where in ("A", "B"):
                return t if where == "A" else t - 1
            return {"out_proj": t, "turn_back": t - 1}.get(name, t + LAYER_GROUP[where])

        def last_reader(key, t):
            name, where, n = key
            g = group_of(name, where, t)
            if name in ("scores", "turn"):
                return (exped if name == "scores" else pt_ready)[where], UNITS * g + n + 1
            if name == "heads":
                return ot_ready[where], GROUP * g + n + 1
            if name == "turn_x":
                return xt_ready[where], KT * g + n + 1
            if name in ("q", "k"):
                return (qt_ready if name == "q" else kt_ready)["A" if where == "0" else "B"], KT * g + n + 1
            if name == "v":
                return v_ready["A" if where == "0" else "B"], GROUP * g + n + 1
            if name == "spread_k":
                return masked[where], GROUP * (g + 1)
            if name == "turn_p":
                return fpt_ready[where], g + 1
            if name == "turn_rows":
                return ac_rows_ready, 2 * g + n + 1
            done = {"out_proj": summed, "turn_back": x3_scaled, "fc": fp_ready.get(where),
                    "mix": {"1": x2_ready, "3": out_ready}.get(where)}[name]
            return done, GROUP * g + n + 1

        def wait_drained(pe, banks, t, *key):
            former, back = banks.before[key]
            if former[0] != "setup":
                pe.wait_ge(*last_reader(former, t - back))

        def cols(n, width=P):
            return slice(n * width, (n + 1) * width)

        block = ctx.enter_context(nc.Block())

        @block.sync
        def _(sp):
            for n in RAW_ORDER:
                sp.dma_start(raw[n], ins[SOURCE[n]].rearrange("(k p) e -> p k e", p=P)).then_inc(raw_landed, 16)

            def spread(stream, g):
                for k in range(KT):
                    sp.wait_ge(kt_ready[stream], KT * g + k + 1)
                    for h in range(HALF):
                        part = slice(h * HEAD_DIM, (h + 1) * HEAD_DIM)
                        sp.dma_start(kt_diag[stream][part, k, :, h, :],
                                     kt[stream][part, k, :].rearrange("p (g n) -> p g n", g=GROUP)
                                     ).then_inc(kd_landed[stream], 16)

            def turn(body, t, banks):
                if body.has_in:
                    if body.has_mid:
                        sp.wait_ge(summed, GROUP * (t + 1))
                    sp.dma_start(x_in[:, :, :], x_dram[t + 1]).then_inc(x_landed, 16)
                    if body.has_mid:
                        sp.wait_ge(penalty_ready["1"], t + 1)
                        sp.wait_ge(adj2_ready, t + 1)
                        sp.wait_ge(penalty_ready["3"], t + 1)
                    sp.dma_start(adj[:, :, :], adj_dram[t + 1]).then_inc(adj_landed, 16)
                    spread("A", t + 1)
                if body.has_tail:
                    sp.wait_ge(out_ready, GROUP * t)
                    sp.dma_start(out_dram[t - 1], x_out[:, :, :]).then_inc(stored, 16)
                if body.has_mid:
                    spread("B", t)

            run(sp, turn)
            sp.wait_ge(stored, 16 * GROUPS)

        @block.gpsimd
        def _(pool):
            pool.memset(ident[:, :], 0.0).then_inc(const_ready, 1)
            pool.wait_ge(const_ready, 1)
            pool.affine_select(out=ident[:, :], in_=ident[:, :], compare_op=ALU.not_equal, fill=1.0,
                               base=0, pattern=[[-1, P]], channel_multiplier=1).then_inc(const_ready, 1)
            for tile, value in ((one, 1.0), (big, PENALTY), (adj_eps, ADJ_EPS), (ln_eps, LN_EPS), (minus_half, -0.5)):
                pool.memset(tile[:, :], value).then_inc(const_ready, 1)
            pool.memset(ac_cols[:, :, :].bitcast(F32), 1.0).then_inc(const_ready, 1)
            for s in "AB":
                pool.memset(kt_diag[s][:, :, :, :, :], 0.0).then_inc(const_ready, 1)

            def everywhere(cell, shape=(P, GROUP, P)):
                return cell[:, :].unsqueeze(2).broadcast_to(list(shape))

            def make_penalty(layer, g):
                pool.tensor_tensor(penalty[layer][:, :, :], everywhere(one), adj[:, :, :], ALU.subtract
                                   ).then_inc(one_minus[layer], 1)
                pool.wait_ge(one_minus[layer], g + 1)
                pool.tensor_tensor(penalty[layer][:, :, :], penalty[layer][:, :, :], everywhere(big), ALU.mult
                                   ).then_inc(penalty_ready[layer], 1)

            def add_row(layer, row_tile, banks):
                key = ("turn_x", layer, KT - 1)
                pool.wait_ge(filled[banks.bank(*key)], banks.after(*key))
                x = resid[layer]
                pool.tensor_tensor(x[:, :, :], x[:, :, :], row_tile[:, :].unsqueeze(1).broadcast_to([P, GROUP, DIM]),
                                   ALU.add).then_inc(x_biased[layer], 1)

            def spread_inverse(u, g_no):
                g, half = divmod(u, 2)
                pool.wait_ge(inverted["A"], UNITS * g_no + u + 1)
                pool.tensor_tensor(inv_wide[:, u % 2, :].rearrange("p (h d) -> p h d", h=HALF),
                                   inv_den["A"][:, g, half * HALF:(half + 1) * HALF].unsqueeze(2).broadcast_to(
                                       [P, HALF, HEAD_DIM]), everywhere(one, (P, HALF, HEAD_DIM)), ALU.mult
                                   ).then_inc(inv_spread, 1)

            def turn(body, t, banks):
                if body.has_mid:
                    for u in range(UNITS):
                        spread_inverse(u, t)
                    if body.has_tail:
                        pool.wait_ge(masked["1"], GROUP * t)
                    make_penalty("1", t)
                    if body.has_tail:
                        pool.wait_ge(weighed["B"], UNITS * t)
                    pool.tensor_tensor(adj_2[:, :, :], adj[:, :, :], everywhere(adj_eps), ALU.add
                                       ).then_inc(adj2_ready, 1)
                    for pair in range(2):
                        gs = slice(2 * pair, 2 * pair + 2)
                        pool.wait_ge(moments_ready, GROUP * t + 2 * pair + 2)
                        pool.tensor_tensor(rstd[:, gs], moments[:, gs, 1], ln_eps[:, :].broadcast_to([P, 2]), ALU.add
                                           ).then_inc(var_ready, 1)
                        pool.wait_ge(var_ready, 2 * t + pair + 1)
                        pool.tensor_tensor(rstd[:, gs], rstd[:, gs], minus_half[:, :].broadcast_to([P, 2]), ALU.pow
                                           ).then_inc(rstd_ready, 1)
                if body.has_tail:
                    pool.wait_ge(x_biased["2"], t)
                    pool.wait_ge(x3_scaled, GROUP * t)
                    pool.tensor_tensor(x_3[:, :, :], x_3[:, :, :], x_2[:, :, :], ALU.add).then_inc(x3_ready, 1)
                    add_row("3", rows["b3"], banks)
                if body.has_mid:
                    if body.has_tail:
                        pool.wait_ge(masked["3"], GROUP * t)
                    make_penalty("3", t)
                    add_row("1", rows["b1"], banks)
                if body.has_in:
                    pool.wait_ge(adj_landed, 16 * (t + 2))
                    if body.has_mid:
                        pool.wait_ge(weighed["A"], UNITS * (t + 1))
                    add_row("0", out_bias, banks)
                    pool.tensor_scalar(adj_0[:, :, :], adj[:, :, :], ADJ_MIN, 1.0, ALU.max, ALU.mult
                                       ).then_inc(adj0_ready, 1)
                if body.has_mid:
                    add_row("2", rows["b2"], banks)

            pool.wait_ge(small_landed, SMALL_DONE)
            pool.wait_ge(setup_dve, SETUP_DONE)
            pool.wait_ge(const_ready, CONSTANTS)
            run(pool, turn)

        @block.scalar
        def _(act):
            for tile, src in small:
                act.dma_start(tile, src).then_inc(small_landed, 16)
            act.wait_ge(raw_landed, 16 * len(RAW_ORDER))

            for n in TURNED:
                for k in range(KT):
                    b = setup.bank("t_" + n, k)
                    act.wait_ge(filled[b], setup.after("t_" + n, k))
                    act.activation(w_hi[n][:, k, 0:DIM], bank[b][:, 0:DIM], ACT.Copy).then_inc(setup_act, 1)
            for k in range(KT):
                b = setup.bank("t_f3", k)
                act.wait_ge(filled[b], setup.after("t_f3", k))
                act.activation(w3_t[:, k, :], bank[b][:, 0:DIM], ACT.Copy
                               ).then_inc(setup_act, 1)
            for n in DIRECT:
                act.activation(w_hi[n][:, :, 0:DIM], raw[n], ACT.Copy).then_inc(setup_act, 1)
            act.wait_ge(small_landed, SMALL_DONE)
            act.activation(w_hi["v2"][:, :, DIM:WIDE], soul_w[:, :, :], ACT.Copy, scale=-1.0).then_inc(setup_act, 1)
            for n in "13":
                for k in range(KT):
                    b = setup.bank("qk" + n, k)
                    act.wait_ge(filled[b], setup.after("qk" + n, k))
                    act.activation(w_hi["f" + n][:, k, DIM:WIDE], bank[b][:, 0:2], ACT.Copy, scale=-1.0
                                   ).then_inc(setup_act, 1)

            def attend(stage, s, u, body, g_no, banks):
                g, half = divmod(u, 2)
                if stage == "weigh":
                    b = banks.bank("scores", s, u)
                    act.wait_ge(maxed[s], UNITS * g_no + u + 1)
                    for h in range(HALF):
                        last = act.activation(e[s][:, u % 2, cols(h)], bank[b][:, cols(h)], ACT.Exp,
                                              bias=neg_max[s][:, u % 2, h:h + 1], scale=-1.0)
                        if h == HALF - 1:
                            last.then_inc(exped[s], 1)
                elif stage == "turn":
                    b = banks.bank("turn", s, u)
                    act.wait_ge(filled[b], banks.after("turn", s, u))
                    act.activation(pt[s][:, u % 2, :], bank[b][:, :], ACT.Copy
                                   ).then_inc(pt_ready[s], 1)
                elif stage == "finish" and half == 1:
                    b = banks.bank("heads", s, g)
                    act.wait_ge(filled[b], banks.after("heads", s, g))
                    if s == "A":
                        act.activation(inv_den_t[:, g % 2, :], bank[b][:, DIM:2 * DIM], ACT.Copy
                                       ).then_inc(inv_t_ready, 1)
                    else:
                        act.activation(ot["B"][:, g, :], bank[b][:, 0:DIM], ACT.Copy
                                       ).then_inc(ot_ready["B"], 1)
                elif stage == "split" and half == 1 and s == "A":
                    act.wait_ge(ot_ready["A"], GROUP * g_no + g + 1)
                    act.activation(ot_hi[:, g, :], ot["A"][:, g % 2, :], ACT.Copy).then_inc(ot_hi_ready, 1)

            def x_hi(layer, banks):
                for k in range(KT):
                    b = banks.bank("turn_x", layer, k)
                    act.wait_ge(filled[b], banks.after("turn_x", layer, k))
                    act.activation(xt_hi[xt_of[layer]][:, k, :], bank[b][:, :], ACT.Copy
                                   ).then_inc(xt_hi_ready[layer], 1)

            def copy_fc(layer, banks):
                for g in range(GROUP):
                    b = banks.bank("fc", layer, g)
                    act.wait_ge(filled[b], banks.after("fc", layer, g))
                    act.activation(fp[layer][:, g, :], bank[b][:, 0:WIDE], ACT.Copy
                                   ).then_inc(fp_ready[layer], 1)

            def exp_fc(layer, g_no):
                act.wait_ge(f_maxed[layer], g_no + 1)
                for g in range(GROUP):
                    last = act.activation(logits[layer][:, g, :], logits[layer][:, g, :], ACT.Exp,
                                          bias=f_neg_max[layer][:, g:g + 1], scale=-1.0,
                                          accum_out=f_den[layer][:, g:g + 1])
                last.then_inc(f_exped[layer], 1)

            def copy_p(layer, banks):
                b = banks.bank("turn_p", layer, 0)
                act.wait_ge(filled[b], banks.after("turn_p", layer, 0))
                act.activation(fpt[layer][:, :, :].rearrange("p g n -> p (g n)"), bank[b][:, :], ACT.Copy
                               ).then_inc(fpt_ready[layer], 1)

            def copy_qk(layer, s, g_no, banks):
                for k in range(KT):
                    b = banks.bank("k", layer, k)
                    act.wait_ge(filled[b], banks.after("k", layer, k))
                    if not (isinstance(g_no, int) and g_no == 0):
                        act.wait_ge(kd_landed[s], 16 * HALF * KT * g_no)
                    act.activation(kt[s][:, k, :], bank[b][:, :], ACT.Identity,
                                   bias=bias_cols["k" + layer][:, k:k + 1]
                                   ).then_inc(kt_ready[s], 1)
                for k in range(KT):
                    b = banks.bank("q", layer, k)
                    act.wait_ge(filled[b], banks.after("q", layer, k))
                    act.activation(qt[s][:, k, :], bank[b][:, :], ACT.Identity,
                                   bias=bias_cols["q" + layer][:, k:k + 1], scale=-SCALE
                                   ).then_inc(qt_ready[s], 1)

            def copy_v(layer, s, width, banks):
                for g in range(GROUP):
                    b = banks.bank("v", layer, g)
                    act.wait_ge(filled[b], banks.after("v", layer, g))
                    act.activation(v[s][:, g, 0:width], bank[b][:, 0:width], ACT.Copy
                                   ).then_inc(v_ready[s], 1)

            def turn(body, t, banks):
                g_of = {"A": t, "B": t - 1}
                for stage, s, u in attention_steps(body.streams):
                    attend(stage, s, u, body, g_of[s], banks)
                if body.has_tail:
                    x_hi("3", banks)
                    copy_fc("3", banks)
                if body.has_mid:
                    x_hi("1", banks)
                    copy_fc("1", banks)
                if body.has_tail:
                    exp_fc("3", t - 1)
                if body.has_in:
                    x_hi("0", banks)
                    copy_qk("0", "A", t + 1, banks)
                if body.has_mid:
                    exp_fc("1", t)
                if body.has_tail:
                    copy_p("3", banks)
                if body.has_mid:
                    copy_p("1", banks)
                if body.has_in:
                    copy_v("0", "A", DIM, banks)
                if body.has_mid:
                    x_hi("2", banks)
                    copy_qk("2", "B", t, banks)
                    copy_v("2", "B", WIDE, banks)
                    for k in range(2):
                        b = banks.bank("turn_rows", "2", k)
                        act.wait_ge(filled[b], banks.after("turn_rows", "2", k))
                        act.activation(ac_rows[k][:, :], bank[b][0:4, :], ACT.Copy
                                       ).then_inc(ac_rows_ready, 1)

            act.wait_ge(setup_dve, SETUP_DONE)
            run(act, turn)

        @block.vector
        def _(dve):
            def low_part(out_tile, src, hi_tile):
                return dve.tensor_tensor(out_tile, src, hi_tile.bitcast(F32), ALU.subtract)

            dve.wait_ge(raw_landed, 16 * len(RAW_ORDER))
            for n in TURNED:
                for k in range(KT):
                    b = setup.bank("t_" + n, k)
                    dve.wait_ge(setup_act, act_step["hi", n, k])
                    low_part(w_lo[n][:, k, 0:DIM], bank[b][:, 0:DIM], w_hi[n][:, k, 0:DIM]
                             ).then_inc(setup_dve, 1)
            for n in DIRECT:
                dve.wait_ge(setup_act, act_step["hi", n, "all"])
                low_part(w_lo[n][:, :, 0:DIM], raw[n], w_hi[n][:, :, 0:DIM]).then_inc(setup_dve, 1)
            dve.wait_ge(small_landed, SMALL_DONE)
            dve.wait_ge(setup_act, act_step["hi", "soul", "all"])
            dve.scalar_tensor_tensor(w_lo["v2"][:, :, DIM:WIDE], soul_w[:, :, :], -1.0,
                                     w_hi["v2"][:, :, DIM:WIDE].bitcast(F32), ALU.mult, ALU.subtract
                                     ).then_inc(setup_dve, 1)
            for n in "13":
                for k in range(KT):
                    b = setup.bank("qk" + n, k)
                    dve.wait_ge(setup_act, act_step["hi", "qk" + n, k])
                    dve.scalar_tensor_tensor(w_lo["f" + n][:, k, DIM:WIDE], bank[b][:, 0:2], -1.0,
                                             w_hi["f" + n][:, k, DIM:WIDE].bitcast(F32), ALU.mult, ALU.subtract
                                             ).then_inc(setup_dve, 1)
            dve.memset(soul_b[:, 1:2], 0.0).then_inc(setup_dve, 1)
            for n in ("q0", "q2"):
                dve.tensor_scalar(bias_cols[n][:, :], bias_cols[n][:, :], -SCALE, None, ALU.mult
                                  ).then_inc(setup_dve, 1)
            dve.wait_ge(setup_dve, dve_step["zero", "", ""])
            dve.tensor_scalar(soul_b[:, :], soul_b[:, :], -1.0, None, ALU.mult).then_inc(setup_dve, 1)
            for n in "13":
                b = setup.bank("c" + n, 0)
                dve.wait_ge(filled[b], setup.after("c" + n, 0))
                dve.tensor_tensor(qk_b[n][:, :], bank[b][:, 0:2], qk_b[n][:, :], ALU.add
                                  ).then_inc(setup_dve, 1)
                dve.wait_ge(setup_dve, dve_step["sum", n, ""])
                dve.tensor_scalar(qk_b[n][:, :], qk_b[n][:, :], -1.0, None, ALU.mult).then_inc(setup_dve, 1)
            b = setup.bank("out_bias", 0)
            dve.wait_ge(filled[b], setup.after("out_bias", 0))
            dve.tensor_tensor(out_bias[:, :], bank[b][:, 0:DIM], out_bias[:, :], ALU.add
                              ).then_inc(setup_dve, 1)

            def attend(stage, s, u, g_no, banks):
                g, half = divmod(u, 2)
                if stage == "scores":
                    b = banks.bank("scores", s, u)
                    dve.wait_ge(filled[b], banks.after("scores", s, u))
                    dve.tensor_reduce(neg_max[s][:, u % 2, :], bank[b][:, :].rearrange("p (h n) -> p h n", h=HALF),
                                      axis=AX.X, op=ALU.min).then_inc(maxed[s], 1)
                elif stage == "weigh":
                    if u == 0:
                        dve.wait_ge(adj0_ready if s == "A" else adj2_ready, g_no + 1)
                    dve.wait_ge(exped[s], UNITS * g_no + u + 1)
                    for h in range(HALF):
                        last = dve.tensor_tensor_reduce(
                            out=pr[s][:, u % 2, cols(h)], in0=e[s][:, u % 2, cols(h)], in1=weight_of[s][:, g, :],
                            scale=1.0, scalar=0.0, op0=ALU.mult, op1=ALU.add,
                            accum_out=den[s][:, u % 2, h:h + 1])
                    last.then_inc(weighed[s], 1)
                elif stage == "turn":
                    dve.wait_ge(weighed[s], UNITS * g_no + u + 1)
                    dve.reciprocal(inv_den[s][:, g, half * HALF:(half + 1) * HALF], den[s][:, u % 2, :]
                                   ).then_inc(inverted[s], 1)
                elif stage == "finish" and half == 1 and s == "A":
                    b = banks.bank("heads", s, g)
                    dve.wait_ge(inv_t_ready, GROUP * g_no + g + 1)
                    dve.tensor_tensor(ot["A"][:, g % 2, :], bank[b][:, 0:DIM], inv_den_t[:, g % 2, :], ALU.mult
                                      ).then_inc(ot_ready["A"], 1)
                elif stage == "split" and half == 1 and s == "A":
                    dve.wait_ge(ot_hi_ready, GROUP * g_no + g + 1)
                    low_part(ot_lo[:, g, :], ot["A"][:, g % 2, :], ot_hi[:, g, :]).then_inc(ot_lo_ready, 1)

            def x_lo(layer, g_no, banks):
                for k in range(KT):
                    b = banks.bank("turn_x", layer, k)
                    dve.wait_ge(xt_hi_ready[layer], KT * g_no + k + 1)
                    s = xt_of[layer]
                    low_part(xt_lo[s][:, k, :], bank[b][:, :], xt_hi[s][:, k, :]
                             ).then_inc(xt_ready[layer], 1)

            def mask(layer, g_no, banks):
                dve.wait_ge(fp_ready[layer], GROUP * (g_no + 1))
                qk = fp[layer][:, :, DIM:WIDE]
                dve.tensor_tensor(qk, qk, qk_b[layer][:, :].unsqueeze(1).broadcast_to([P, GROUP, 2]), ALU.add
                                  ).then_inc(qk_ready[layer], 1)
                b = banks.bank("spread_k", layer, 0)
                dve.wait_ge(penalty_ready[layer], g_no + 1)
                dve.wait_ge(filled[b], banks.after("spread_k", layer, 0))
                for g in range(GROUP):
                    dve.scalar_tensor_tensor(logits[layer][:, g, :], bank[b][:, cols(g)],
                                             fp[layer][:, g, DIM:DIM + 1], penalty[layer][:, g, :],
                                             ALU.add, ALU.add).then_inc(masked[layer], 1)
                dve.wait_ge(masked[layer], GROUP * (g_no + 1))
                dve.scalar_tensor_tensor(logits[layer][:, :, :], logits[layer][:, :, :], SLOPE,
                                         logits[layer][:, :, :], ALU.mult, ALU.min).then_inc(leaked[layer], 1)
                dve.wait_ge(leaked[layer], g_no + 1)
                dve.tensor_reduce(f_neg_max[layer][:, :], logits[layer][:, :, :], axis=AX.X, op=ALU.min
                                  ).then_inc(f_maxed[layer], 1)

            def residual(layer, g_no, result, ready, banks):
                dve.wait_ge(f_exped[layer], g_no + 1)
                dve.reciprocal(f_inv[layer][:, :], f_den[layer][:, :]).then_inc(f_inverted[layer], 1)
                dve.wait_ge(f_inverted[layer], g_no + 1)
                dve.wait_ge(x_biased[layer], g_no + 1)
                for g in range(GROUP):
                    b = banks.bank("mix", layer, g)
                    dve.wait_ge(filled[b], banks.after("mix", layer, g))
                    dve.scalar_tensor_tensor(result[:, g, :], bank[b][:, 0:DIM], f_inv[layer][:, g:g + 1],
                                             resid[layer][:, g, :], ALU.mult, ALU.add
                                             ).then_inc(ready, 1)

            def turn(body, t, banks):
                g_of = {"A": t, "B": t - 1}
                for stage, s, u in attention_steps(body.streams):
                    attend(stage, s, u, g_of[s], banks)
                if body.has_mid:
                    dve.wait_ge(x_biased["0"], t + 1)
                    for i in range(GROUP + 1):
                        if i < GROUP:
                            b = banks.bank("out_proj", "0", i)
                            dve.wait_ge(filled[b], banks.after("out_proj", "0", i))
                            dve.tensor_tensor(x_1[:, i, :], bank[b][:, 0:DIM], x_in[:, i, :], ALU.add
                                              ).then_inc(summed, 1)
                        if i >= 1:
                            dve.wait_ge(summed, GROUP * t + i)
                            if i >= 2:
                                dve.wait_ge(stats_ready, GROUP * t + i - 1)
                            dve.bn_stats(stats[:, i - 1, :], x_1[:, i - 1, :]).then_inc(stats_ready, 1)
                        if i >= 2:
                            dve.bn_aggr(moments[:, i - 2, :], stats[:, i - 2, :]).then_inc(moments_ready, 1)
                if body.has_tail:
                    for g in range(GROUP):
                        b = banks.bank("turn_back", "2", g)
                        if g == 0:
                            dve.wait_ge(inverted["B"], UNITS * t)
                        dve.wait_ge(filled[b], banks.after("turn_back", "2", g))
                        dve.tensor_tensor(
                            x_3[:, g, :].rearrange("p (h d) -> p h d", h=HEADS),
                            bank[b][:, 0:DIM].rearrange("p (h d) -> p h d", h=HEADS),
                            inv_den["B"][:, g, :].unsqueeze(2).broadcast_to([P, HEADS, HEAD_DIM]), ALU.mult
                        ).then_inc(x3_scaled, 1)
                if body.has_mid:
                    for i in range(GROUP + 1):
                        if i < GROUP:
                            dve.wait_ge(moments_ready, GROUP * t + i + 1)
                            if i == 0:
                                dve.wait_ge(stats_ready, GROUP * (t + 1))
                            dve.scalar_tensor_tensor(x_1[:, i, :], x_1[:, i, :], moments[:, i, 0:1],
                                                     rows["gamma"][:, :], ALU.subtract, ALU.mult
                                                     ).then_inc(centred, 1)
                            if i == 0:
                                dve.bn_aggr(moments[:, GROUP - 1, :], stats[:, GROUP - 1, :]
                                            ).then_inc(moments_ready, 1)
                        if i >= 1:
                            dve.wait_ge(centred, GROUP * t + i)
                            dve.wait_ge(rstd_ready, 2 * t + (i - 1) // 2 + 1)
                            dve.scalar_tensor_tensor(x_1[:, i - 1, :], x_1[:, i - 1, :], rstd[:, i - 1:i],
                                                     rows["beta"][:, :], ALU.mult, ALU.add
                                                     ).then_inc(x1_ready, 1)
                if body.has_tail:
                    x_lo("3", t - 1, banks)
                    mask("3", t - 1, banks)
                if body.has_mid:
                    x_lo("1", t, banks)
                    mask("1", t, banks)
                if body.has_in:
                    x_lo("0", t + 1, banks)
                if body.has_tail:
                    residual("3", t - 1, x_out, out_ready, banks)
                if body.has_mid:
                    residual("1", t, x_2, x2_ready, banks)
                    x_lo("2", t, banks)
                    dve.wait_ge(v_ready["B"], GROUP * (t + 1))
                    dve.tensor_tensor(ac_sum[:, :, :], v["B"][:, :, DIM:WIDE],
                                      soul_b[:, :].unsqueeze(1).broadcast_to([P, GROUP, 2]), ALU.add
                                      ).then_inc(ac_summed, 1)
                    dve.wait_ge(ac_summed, t + 1)
                    dve.tensor_copy(ac_cols[:, :, 0:7:6], ac_sum[:, :, :]).then_inc(ac_hi_ready, 1)
                    if body.has_tail:
                        dve.wait_ge(stored, 16 * t)
                    dve.wait_ge(ac_hi_ready, t + 1)
                    low_part(ac_cols[:, :, 1:8:6], ac_sum[:, :, :], ac_cols[:, :, 0:7:6]).then_inc(ac_ready, 1)

            dve.wait_ge(setup_dve, SETUP_DONE)
            dve.wait_ge(const_ready, CONSTANTS)
            run(dve, turn)

        @block.tensor
        def _(pe):
            def three_pass(out_ap, left_hi, left_lo, right_hi, right_lo):
                for k in range(KT):
                    pe.matmul(out_ap, left_hi(k), right_hi(k), start=(k == 0), stop=False)
                    pe.matmul(out_ap, left_lo(k), right_hi(k), start=False, stop=False)
                    last = pe.matmul(out_ap, left_hi(k), right_lo(k), start=False, stop=(k == KT - 1))
                return last

            def drained_setup(*key):
                if setup.before[key] is not None:
                    name, k = setup.before[key][0]
                    if name == "t_f3":
                        pe.wait_ge(setup_act, act_step["w3_t", "", k])
                    else:
                        pe.wait_ge(setup_dve, dve_step["lo", name[2:] if name[:2] == "t_" else name, k])

            pe.wait_ge(raw_landed, 16 * len(RAW_ORDER))
            pe.wait_ge(const_ready, 2)
            for n in TURNED + ("f3",):
                for k in range(KT):
                    b = setup.bank("t_" + n, k)
                    drained_setup("t_" + n, k)
                    for j in range(KT):
                        last = pe.transpose(bank[b][:, cols(j)], raw[n][:, j, cols(k)], ident[:, :])
                    last.then_inc(filled[b], 1)
            pe.wait_ge(small_landed, SMALL_DONE)
            for n in "13":
                if n == "3":
                    pe.wait_ge(setup_act, act_step["w3_t", "", KT - 1])
                by_row = raw["f1"] if n == "1" else w3_t
                for k in range(KT):
                    b = setup.bank("qk" + n, k)
                    drained_setup("qk" + n, k)
                    for j in range(KT):
                        last = pe.matmul(bank[b][:, 0:2], by_row[:, j, cols(k)], qk_w[n][:, j, :],
                                         start=(j == 0), stop=(j == KT - 1))
                    last.then_inc(filled[b], 1)
            for n in "13":
                b = setup.bank("c" + n, 0)
                drained_setup("c" + n, 0)
                for j in range(KT):
                    last = pe.matmul(bank[b][:, 0:2], fc_bias_col[n][:, j:j + 1].broadcast_to([P, P]),
                                     qk_w[n][:, j, :], start=(j == 0), stop=(j == KT - 1))
                last.then_inc(filled[b], 1)
            b = setup.bank("out_bias", 0)
            drained_setup("out_bias", 0)
            pe.wait_ge(setup_dve, dve_step["lo", "o0", KT - 1])
            for j in range(KT):
                for part in (w_hi, w_lo):
                    last = pe.matmul(bank[b][:, 0:DIM], bv_col[:, j:j + 1].broadcast_to([P, P]),
                                     part["o0"][:, j, 0:DIM].bitcast(F32), start=(j == 0 and part is w_hi),
                                     stop=(j == KT - 1 and part is w_lo))
            last.then_inc(filled[b], 1)

            def scores(s, u, g_no, t, banks):
                g, half = divmod(u, 2)
                b = banks.bank("scores", s, u)
                if u == 0:
                    pe.wait_ge(qt_ready[s], KT * (g_no + 1))
                    pe.wait_ge(kd_landed[s], 16 * HALF * KT * (g_no + 1))
                    if s == "B":
                        pe.wait_ge(ac_rows_ready, 2 * (g_no + 1))
                wait_drained(pe, banks, t, "scores", s, u)
                last = pe.matmul(bank[b][:, :], qt[s][:, half, cols(g)], kt_diag[s][:, half, g, :, :],
                                 start=True, stop=(s == "A"))
                if s == "B":
                    last = pe.matmul(bank[b][:, :], ac_rows[0][:, cols(g)],
                                     ac_rows[1][:, cols(g)].unsqueeze(1).broadcast_to([4, HALF, P]),
                                     start=False, stop=True)
                last.then_inc(filled[b], 1)

            def turn_probabilities(s, u, g_no, t, banks):
                b = banks.bank("turn", s, u)
                pe.wait_ge(weighed[s], UNITS * g_no + u + 1)
                wait_drained(pe, banks, t, "turn", s, u)
                for h in range(HALF):
                    last = pe.transpose(bank[b][:, cols(h)], pr[s][:, u % 2, cols(h)], ident[:, :])
                last.then_inc(filled[b], 1)

            def use(s, u, g_no, t, banks):
                g, half = divmod(u, 2)
                b = banks.bank("heads", s, g)
                if half == 0:
                    wait_drained(pe, banks, t, "heads", s, g)
                if u == 0:
                    pe.wait_ge(v_ready[s], GROUP * (g_no + 1))
                pe.wait_ge(pt_ready[s], UNITS * g_no + u + 1)
                for h in range(HALF):
                    head = (half * HALF + h) * HEAD_DIM
                    part = slice(h * HEAD_DIM, (h + 1) * HEAD_DIM)
                    last = pe.matmul(bank[b][part, cols(half)], v[s][:, g, head:head + HEAD_DIM],
                                     pt[s][:, u % 2, cols(h)], start=True, stop=True)
                if s == "A":
                    pe.wait_ge(inv_spread, UNITS * g_no + u + 1)
                    last = pe.transpose(bank[b][:, cols(2 + half)], inv_wide[:, u % 2, :], ident[:, :])
                if half == 1:
                    last.then_inc(filled[b], 1)

            X_READY = {"0": (x_landed, 16), "1": (x1_ready, GROUP), "2": (x2_ready, GROUP), "3": (x3_ready, 1)}

            def step(name, layer, n, g_no, t, banks):
                b = banks.bank(name, layer, n)
                to = bank[b]
                s = xt_of[layer]
                wait_drained(pe, banks, t, name, layer, n)
                if name == "turn_x":
                    ready, per_group = X_READY[layer]
                    pe.wait_ge(ready, per_group * (g_no + 1))
                    for g in range(GROUP):
                        last = pe.transpose(to[:, cols(g)], resid[layer][:, g, cols(n)], ident[:, :])
                elif name in ("q", "k"):
                    pe.wait_ge(xt_ready[layer], KT * (g_no + 1))
                    w = name + layer
                    last = three_pass(to[:, :], lambda k: w_hi[w][:, k, cols(n)], lambda k: w_lo[w][:, k, cols(n)],
                                      lambda k: xt_hi[s][:, k, :], lambda k: xt_lo[s][:, k, :])
                elif name in ("v", "fc"):
                    pe.wait_ge(xt_ready[layer], KT * (g_no + 1))
                    w = name[0] + layer
                    width = DIM if layer == "0" else WIDE
                    last = three_pass(to[:, 0:width],
                                      lambda k: xt_hi[s][:, k, cols(n)], lambda k: xt_lo[s][:, k, cols(n)],
                                      lambda k: w_hi[w][:, k, 0:width], lambda k: w_lo[w][:, k, 0:width])
                elif name == "out_proj":
                    pe.wait_ge(ot_lo_ready, GROUP * g_no + n + 1)
                    last = three_pass(to[:, 0:DIM],
                                      lambda k: ot_hi[:, n, cols(k)], lambda k: ot_lo[:, n, cols(k)],
                                      lambda k: w_hi["o0"][:, k, 0:DIM], lambda k: w_lo["o0"][:, k, 0:DIM])
                elif name == "turn_back":
                    pe.wait_ge(ot_ready["B"], GROUP * g_no + n + 1)
                    for k in range(KT):
                        last = pe.transpose(to[:, cols(k)], ot["B"][:, n, cols(k)], ident[:, :])
                elif name == "spread_k":
                    pe.wait_ge(qk_ready[layer], g_no + 1)
                    for g in range(GROUP):
                        last = pe.transpose(to[:, cols(g)], fp[layer][:, g, DIM + 1:WIDE].broadcast_to([P, P]),
                                            ident[:, :])
                elif name == "turn_p":
                    pe.wait_ge(f_exped[layer], g_no + 1)
                    for g in range(GROUP):
                        last = pe.transpose(to[:, cols(g)], logits[layer][:, g, :], ident[:, :])
                elif name == "mix":
                    pe.wait_ge(fpt_ready[layer], g_no + 1)
                    last = pe.matmul(to[:, 0:DIM], fpt[layer][:, n, :], fp[layer][:, n, 0:DIM], start=True, stop=True)
                else:
                    assert name == "turn_rows"
                    pe.wait_ge(ac_ready, g_no + 1)
                    for g in range(GROUP):
                        last = pe.transpose(to[0:4, cols(g)], ac_cols[:, g, 4 * n:4 * n + 4].bitcast(F32), ident[:, :])
                last.then_inc(filled[b], 1)

            ATTENTION = {"scores": scores, "turn": turn_probabilities, "use": use}

            def turn(body, t, banks):
                for name, where, n in body.tensor_steps():
                    g_no = group_of(name, where, t)
                    if name in ATTENTION:
                        ATTENTION[name](where, n, g_no, t, banks)
                    else:
                        step(name, where, n, g_no, t, banks)

            pe.wait_ge(setup_dve, SETUP_DONE)
            pe.wait_ge(const_ready, CONSTANTS)
            run(pe, turn)


INPUTS = ["x", "adj", "L0_gnn_Wq", "L0_gnn_bq", "L0_gnn_Wk", "L0_gnn_bk", "L0_gnn_Wv", "L0_gnn_bv", "L0_gnn_Wo",
          "L0_gnn_bo", "L0_gnn_gamma", "L0_gnn_beta", "L1_gnn_fc_w", "L1_gnn_fc_b", "L1_gnn_q_w", "L1_gnn_q_b",
          "L1_gnn_k_w", "L1_gnn_k_b", "L2_gnn_W_q", "L2_gnn_b_q", "L2_gnn_W_k", "L2_gnn_b_k", "L2_gnn_W_v",
          "L2_gnn_b_v", "L2_gnn_w_g", "L2_gnn_b_g", "L3_gnn_W_fc", "L3_gnn_b_fc", "L3_gnn_w_q", "L3_gnn_b_q",
          "L3_gnn_w_k", "L3_gnn_b_k"]


def kernel(**inputs):
    import numpy as np
    import concourse.bacc as bacc
    from concourse.bass_utils import run_bass_kernel_spmd

    nc = bacc.Bacc("TRN2", target_bir_lowering=False, num_devices=1)
    arrays, ins = {}, {}
    for name in INPUTS:
        a = np.ascontiguousarray(inputs[name])
        if name == "L2_gnn_b_g":
            a = a.reshape(1)
        arrays[name + "_dram"] = a
        ins[name] = nc.dram_tensor(name + "_dram", a.shape, mybir.dt.from_np(a.dtype), kind="ExternalInput").ap()
    out = nc.dram_tensor("out_dram", arrays["x_dram"].shape, F32, kind="ExternalOutput").ap()
    build_kernel(nc, ins, out)
    result = run_bass_kernel_spmd(nc, [arrays], core_ids=[0])
    return result.results[0]["out_dram"]
```

```python
import concourse.bass as bass
from concourse import mybir
from contextlib import ExitStack

F32 = mybir.dt.float32
F32R = mybir.dt.float32r
ALU = mybir.AluOpType
ACT = mybir.ActivationFunctionType
AX = mybir.AxisListType

P = 128
GROUP = 2
HEADS, HEAD_DIM = 8, 32
HALF = 4
UNITS = GROUP * 2
KT = 2
BANKS = 8
ADJ_MIN, ADJ_EPS, LN_EPS, PENALTY, SLOPE = 1e-8, 1e-9, 1e-5, 1e9, 0.01
SCALE = 1.0 / float(HEAD_DIM) ** 0.5

SLOTS = 8
ATTEND_AT = {"A": 4, "B": 31}
SCORE_BANK = {"A": 0, "B": 1}
HEADS_BANK = {"A": 2, "B": 3}
OTHER_BANKS = (4, 5, 6, 7)

ATTEND = {
    "A": {"scores": 0, "weigh": 1.0, "turn": 2.36, "use": 3.5, "finish": 4.6, "split": 5.7, "out_proj": 6.22},
    "B": {"scores": -0.42, "weigh": 1.06, "turn": 2.35, "use": 3.5, "finish": 4.6, "turn_back": 5.19},
}


def plan():
    steps = [(-5, "load", "", 0), (-0.12, "turn_x", "0", 0), (0.34, "bias", "0", 0), (1.0, "adj_0", "", 0),
             (1.45, "k", "0", 0), (1.74, "spread", "A", 0), (2.1, "q", "0", 0), (3.71, "v", "0", 0),
             (10.46, "adj_m", "", 0), (16.1, "penalty", "1", 0), (16.9, "rstd", "", 0), (17.4, "norm", "", 0),
             (19.84, "turn_x", "1", 0), (20.27, "bias", "1", 0), (20.36, "fc", "1", 0), (21.45, "fc", "1", 1),
             (21.8, "qk", "1", 0), (22.3, "mask", "1", 0), (23.1, "exp", "1", 0), (24.1, "turn_p", "1", 0),
             (25.1, "mix", "1", 0), (25.2, "adj_2", "", 0), (25.3, "adj_n", "", 0), (26.36, "turn_x", "2", 0),
             (26.78, "bias", "2", 0), (27.1, "k", "2", 0), (27.14, "spread", "B", 0), (28.1, "q", "2", 0),
             (29.1, "v", "2", 0), (29.45, "v", "2", 1), (29.7, "ac", "2", 0), (30.1, "turn_rows", "2", 0),
             (40.75, "penalty", "3", 0), (42.3, "x_3", "", 0), (46.1, "turn_x", "3", 0), (46.3, "bias", "3", 0),
             (47.1, "fc", "3", 0), (47.45, "fc", "3", 1), (47.8, "qk", "3", 0), (48.1, "mask", "3", 0),
             (49.1, "exp", "3", 0), (50.43, "turn_p", "3", 0), (51.1, "mix", "3", 0), (51.9, "store", "", 0)]
    for s, start in ATTEND_AT.items():
        for name, later in ATTEND[s].items():
            if name in ("scores", "weigh", "turn", "use"):
                steps += [(start + 2 * u + later, name, s, u) for u in range(UNITS)]
            else:
                where = {"out_proj": "0", "turn_back": "2"}.get(name, s)
                steps += [(start + 2 * (2 * g + 1) + later, name, where, g) for g in range(GROUP)]
    return steps


LATER = {
    ("scalar", "q", "2"): 0.12, ("scalar", "split", "A"): -0.38, ("scalar", "v", "2"): 0.28,
    ("scalar", "weigh", "A"): -0.25, ("vector", "finish", "A"): -0.07, ("vector", "mask", "3"): 0.05,
    ("vector", "turn", "B"): 0.33, ("vector", "turn_x", "2"): 0.15,
}


def order(engine):
    timed = [(at + LATER.get((engine, name, where), 0), name, where, n) for at, name, where, n in plan()]
    return [(int(at // SLOTS), name, where, n) for at, name, where, n in sorted(timed, key=lambda step: step[0] % SLOTS)]


ENGINES = ("tensor", "vector", "scalar", "gpsimd", "sync")
ORDER = {engine: order(engine) for engine in ENGINES}
LAG = {(name, where, n): lag for lag, name, where, n in ORDER["tensor"]}
ALL_LAGS = [lag for engine in ENGINES for lag, *_ in ORDER[engine]]
FIRST_LAG, LAST_LAG = min(ALL_LAGS), max(ALL_LAGS)
OTHERS_NAMES = ("turn", "turn_x", "k", "q", "v", "fc", "mask", "turn_p", "mix", "turn_rows", "out_proj", "turn_back")
OTHERS = [(name, where, n) for _, name, where, n in ORDER["tensor"] if name in OTHERS_NAMES]
OTHER_BANK = {key: OTHER_BANKS[i % len(OTHER_BANKS)] for i, key in enumerate(OTHERS)}


class Group:

    def __init__(self, no, odd):
        self.no, self.odd = no, odd

    def wait_former(self, engine, semaphore, per_group, back):
        value = per_group * (self.no - back + 1)
        if not isinstance(value, int) or value > 0:
            engine.wait_ge(semaphore, value)


class Setup:

    def __init__(self, fills):
        self.place, self.before, self.count = {}, {}, [0] * BANKS
        held = {}
        for key, bank in fills:
            self.before[key] = held.get(bank)
            self.count[bank] += 1
            self.place[key] = (bank, self.count[bank])
            held[bank] = key

    def bank(self, *key):
        return self.place[key][0]

    def after(self, *key):
        return self.place[key][1]


class Turn:

    def __init__(self, t, odd, active, start, held):
        self.t, self.odd, self.active, self.start = t, odd, active, start
        self.place, self.before = {}, {}
        self.count = [0] * BANKS
        held = dict(held)
        for key, bank in self.fills():
            self.place[key] = (bank, self.count[bank])
            self.before[key] = held.get(bank)
            self.count[bank] += 1
            held[bank] = (key, 0)
        self.held = {b: (key, back + 1) for b, (key, back) in held.items()}

    def group(self, lag):
        return Group(self.t - lag, (self.odd - lag) % 2)

    def steps(self, engine):
        for lag, name, where, n in ORDER[engine]:
            if lag in self.active:
                yield name, where, n, self.group(lag)

    def fills(self):
        for name, where, n, _ in self.steps("tensor"):
            if name == "scores":
                yield (name, where, n), SCORE_BANK[where]
            elif (name, where, n) in OTHER_BANK:
                yield (name, where, n), OTHER_BANK[name, where, n]

    def bank(self, *key):
        return self.place[key][0]

    def after(self, *key):
        bank, n = self.place[key]
        return self.start[bank] + n + 1


def build_kernel(nc, ins, out):
    GRAPHS, NODES, DIM = ins["x"].shape
    assert NODES == P and DIM == KT * P and GRAPHS % GROUP == 0
    GROUPS = GRAPHS // GROUP
    WIDE = DIM + 2
    x_dram = ins["x"].rearrange("(t g) n d -> t n g d", g=GROUP)
    adj_dram = ins["adj"].rearrange("(t g) n m -> t n g m", g=GROUP)
    out_dram = out.rearrange("(t g) n d -> t n g d", g=GROUP)

    with ExitStack() as ctx:
        def sb(name, shape, dt=F32):
            return ctx.enter_context(nc.sbuf_tensor(name, shape, dt))

        def sem(name):
            return ctx.enter_context(nc.semaphore(name))

        ctx.enter_context(nc.allow_non_contiguous_dma(reason="weight columns, once"))

        bank = [ctx.enter_context(nc.psum_tensor(f"bank{b}", [P, 512], F32)) for b in range(BANKS)]
        filled = [sem(f"filled{b}") for b in range(BANKS)]

        x_in = sb("x_in", [P, GROUP, DIM])
        x_0 = sb("x_0", [P, 2, GROUP, DIM])
        x_1 = sb("x_1", [P, 2, GROUP, DIM])
        x_2 = sb("x_2", [P, GROUP, DIM])
        x_2b = sb("x_2b", [P, 2, GROUP, DIM])
        x_3 = sb("x_3", [P, 2, GROUP, DIM])
        x_out = sb("x_out", [P, GROUP, DIM])
        adj = sb("adj", [P, 2, GROUP, P])
        adj_m = sb("adj_m", [P, 2, GROUP, P])
        adj_n = sb("adj_n", [P, 2, GROUP, P])
        adj_0 = sb("adj_0", [P, 2, GROUP, P])
        adj_2 = sb("adj_2", [P, 2, GROUP, P])
        penalty = {n: sb(f"penalty_{n}", [P, GROUP, P]) for n in "13"}
        weight_of = {"A": adj_0, "B": adj_2}

        xt_hi = {n: sb(f"xt_hi_{n}", [P, KT, GROUP * P], F32R) for n in "0123"}
        xt_lo = {n: sb(f"xt_lo_{n}", [P, KT, GROUP * P], F32R) for n in "0123"}

        qt = {s: sb(f"qt_{s}", [P, 2, KT, GROUP * P]) for s in "AB"}
        kt = {s: sb(f"kt_{s}", [P, KT, GROUP * P]) for s in "AB"}
        kt_diag = {s: sb(f"kt_diag_{s}", [P, 2, KT, GROUP, HALF, P]) for s in "AB"}
        v = {"A": sb("v_A", [P, 2, GROUP, DIM]), "B": sb("v_B", [P, 2, GROUP, WIDE])}
        scratch = sb("scratch", [P, 6, 2, HALF * P])
        e = {s: scratch[:, 3 * n + 0] for n, s in enumerate("AB")}
        pr = {s: scratch[:, 3 * n + 1] for n, s in enumerate("AB")}
        pt = {s: scratch[:, 3 * n + 2] for n, s in enumerate("AB")}
        neg_max = {s: sb(f"neg_max_{s}", [P, 2, HALF]) for s in "AB"}
        den = {s: sb(f"den_{s}", [P, 2, HALF]) for s in "AB"}
        inv_den = {s: sb(f"inv_den_{s}", [P, 2, GROUP, HEADS]) for s in "AB"}
        inv_wide = sb("inv_wide", [P, 2, P])
        inv_den_t = sb("inv_den_t", [P, GROUP, DIM])
        ot = {s: sb(f"ot_{s}", [P, GROUP, DIM]) for s in "AB"}
        ot_hi = sb("ot_hi", [P, GROUP, DIM], F32R)
        ot_lo = sb("ot_lo", [P, GROUP, DIM], F32R)
        ac_sum = sb("ac_sum", [P, GROUP, 2])
        ac_cols = sb("ac_cols", [P, GROUP, 8], F32R)
        ac_rows = sb("ac_rows", [4, 2, GROUP * P], F32R)

        fp = {n: sb(f"fp_{n}", [P, GROUP, WIDE]) for n in "13"}
        logits = {n: sb(f"logits_{n}", [P, GROUP, P]) for n in "13"}
        fpt = {n: sb(f"fpt_{n}", [P, GROUP, P]) for n in "13"}
        f_neg_max = {n: sb(f"f_neg_max_{n}", [P, GROUP]) for n in "13"}
        f_den = {n: sb(f"f_den_{n}", [P, GROUP]) for n in "13"}
        f_inv = {n: sb(f"f_inv_{n}", [P, GROUP]) for n in "13"}

        stats = sb("stats", [P, GROUP, 6])
        moments = sb("moments", [P, GROUP, 2])
        rstd = sb("rstd", [P, GROUP])
        one, big, adj_eps, ln_eps, minus_half = (
            sb(name, [P, 1]) for name in ("one", "big", "adj_eps", "ln_eps", "minus_half"))

        ident = sb("ident", [P, P])
        w_hi = {n: sb(f"w_hi_{n}", [P, KT, WIDE], F32R) for n in ("q0", "k0", "v0", "o0", "f1", "q2", "k2", "v2", "f3")}
        w_lo = {n: sb(f"w_lo_{n}", [P, KT, WIDE], F32R) for n in w_hi}
        SOURCE = {"q0": "L0_gnn_Wq", "k0": "L0_gnn_Wk", "v0": "L0_gnn_Wv", "o0": "L0_gnn_Wo", "f1": "L1_gnn_fc_w",
                  "q2": "L2_gnn_W_q", "k2": "L2_gnn_W_k", "v2": "L2_gnn_W_v", "f3": "L3_gnn_W_fc"}
        RAW_ORDER = list(SOURCE)
        flat = scratch[:, :, :, :].rearrange("p a b c -> p (a b c)")
        raw = {n: flat[:, i * 512:(i + 1) * 512].rearrange("p (k e) -> p k e", k=KT) for i, n in enumerate(RAW_ORDER)}
        w3_t = flat[:, 9 * 512:10 * 512].rearrange("p (k e) -> p k e", k=KT)
        bias_cols = {n: sb(f"bias_{n}", [P, KT]) for n in ("q0", "k0", "q2", "k2")}
        bv_col = sb("bv_col", [P, KT])
        fc_bias_col = {n: sb(f"fc_bias_col_{n}", [P, KT]) for n in "13"}
        qk_w = {n: sb(f"qk_w_{n}", [P, KT, 2]) for n in "13"}
        qk_b = {n: sb(f"qk_b_{n}", [P, 2]) for n in "13"}
        soul_w = sb("soul_w", [P, KT, 2])
        soul_b = sb("soul_b", [P, 2])
        rows = {n: sb(f"row_{n}", [P, DIM]) for n in ("gamma", "beta", "b1", "b2", "b3")}
        out_bias = sb("out_bias", [P, DIM])

        CONSTANTS = 10

        x_landed, adj_landed, stored = sem("x_landed"), sem("adj_landed"), sem("stored")
        kd_landed = {s: sem(f"kd_landed_{s}") for s in "AB"}
        raw_landed, small_landed = sem("raw_landed"), sem("small_landed")
        const_ready = sem("const_ready")
        setup_act, setup_dve = sem("setup_act"), sem("setup_dve")
        xt_hi_ready = {n: sem(f"xt_hi_ready_{n}") for n in "0123"}
        xt_ready = {n: sem(f"xt_ready_{n}") for n in "0123"}
        qt_ready = {s: sem(f"qt_ready_{s}") for s in "AB"}
        kt_ready = {s: sem(f"kt_ready_{s}") for s in "AB"}
        v_ready = {s: sem(f"v_ready_{s}") for s in "AB"}
        V_PARTS = {"A": 1, "B": GROUP}
        maxed = {s: sem(f"maxed_{s}") for s in "AB"}
        exped = {s: sem(f"exped_{s}") for s in "AB"}
        weighed = {s: sem(f"weighed_{s}") for s in "AB"}
        inverted = {s: sem(f"inverted_{s}") for s in "AB"}
        pt_ready = {s: sem(f"pt_ready_{s}") for s in "AB"}
        inv_spread = sem("inv_spread")
        heads_ready = {s: sem(f"heads_ready_{s}") for s in "AB"}
        inv_t_ready = sem("inv_t_ready")
        ot_ready = {s: sem(f"ot_ready_{s}") for s in "AB"}
        ot_hi_ready, ot_lo_ready = sem("ot_hi_ready"), sem("ot_lo_ready")
        summed, stats_ready, moments_ready = sem("summed"), sem("stats_ready"), sem("moments_ready")
        var_ready, rstd_ready = sem("var_ready"), sem("rstd_ready")
        centred, x1_ready = sem("centred"), sem("x1_ready")
        x2_ready, x3_scaled = sem("x2_ready"), sem("x3_scaled")
        x3_ready = sem("x3_ready")
        x_biased = {n: sem(f"x_biased_{n}") for n in "0123"}
        out_ready = sem("out_ready")
        fp_ready = {n: sem(f"fp_ready_{n}") for n in "13"}
        qk_ready = {n: sem(f"qk_ready_{n}") for n in "13"}
        masked = {n: sem(f"masked_{n}") for n in "13"}
        leaked = {n: sem(f"leaked_{n}") for n in "13"}
        f_maxed = {n: sem(f"f_maxed_{n}") for n in "13"}
        f_exped = {n: sem(f"f_exped_{n}") for n in "13"}
        f_inverted = {n: sem(f"f_inverted_{n}") for n in "13"}
        fpt_ready = {n: sem(f"fpt_ready_{n}") for n in "13"}
        adj0_ready, adj2_ready = sem("adj0_ready"), sem("adj2_ready")
        adj_m_ready, adj_n_ready = sem("adj_m_ready"), sem("adj_n_ready")
        one_minus = {n: sem(f"one_minus_{n}") for n in "13"}
        penalty_ready = {n: sem(f"penalty_ready_{n}") for n in "13"}
        ac_summed, ac_hi_ready, ac_ready, ac_rows_ready = (
            sem("ac_summed"), sem("ac_hi_ready"), sem("ac_ready"), sem("ac_rows_ready"))

        def column(name):
            return ins[name].rearrange("(k p) -> p k", p=P)

        def row(name):
            return ins[name].partition_broadcast(P)

        small = [(bias_cols["q0"][:, :], column("L0_gnn_bq")), (bias_cols["k0"][:, :], column("L0_gnn_bk")),
                 (bias_cols["q2"][:, :], column("L2_gnn_b_q")), (bias_cols["k2"][:, :], column("L2_gnn_b_k")),
                 (bv_col[:, :], column("L0_gnn_bv")),
                 (fc_bias_col["1"][:, :], column("L1_gnn_fc_b")), (fc_bias_col["3"][:, :], column("L3_gnn_b_fc")),
                 (qk_w["1"][:, :, 0], ins["L1_gnn_q_w"].rearrange("a (k p) -> p (a k)", p=P)),
                 (qk_w["1"][:, :, 1], ins["L1_gnn_k_w"].rearrange("a (k p) -> p (a k)", p=P)),
                 (qk_w["3"][:, :, 0], ins["L3_gnn_w_q"].rearrange("(k p) a -> p (k a)", p=P)),
                 (qk_w["3"][:, :, 1], ins["L3_gnn_w_k"].rearrange("(k p) a -> p (k a)", p=P)),
                 (qk_b["1"][:, 0:1], row("L1_gnn_q_b")), (qk_b["1"][:, 1:2], row("L1_gnn_k_b")),
                 (qk_b["3"][:, 0:1], row("L3_gnn_b_q")), (qk_b["3"][:, 1:2], row("L3_gnn_b_k")),
                 (soul_w[:, :, 0], ins["L2_gnn_w_g"].rearrange("(c k p) -> c p k", p=P, k=KT)[0]),
                 (soul_w[:, :, 1], ins["L2_gnn_w_g"].rearrange("(c k p) -> c p k", p=P, k=KT)[1]),
                 (soul_b[:, 0:1], ins["L2_gnn_b_g"].partition_broadcast(P)),
                 (out_bias[:, :], row("L0_gnn_bo")), (rows["gamma"][:, :], row("L0_gnn_gamma")),
                 (rows["beta"][:, :], row("L0_gnn_beta")), (rows["b1"][:, :], row("L1_gnn_fc_b")),
                 (rows["b2"][:, :], row("L2_gnn_b_v")), (rows["b3"][:, :], row("L3_gnn_b_fc"))]
        SMALL_DONE = 16 * len(small)

        TURNED, DIRECT = ("q0", "k0", "v0", "o0", "f1"), ("q2", "k2", "v2", "f3")
        both = range(KT)
        ACT_STEPS = ([("hi", n, k) for n in TURNED for k in both] + [("w3_t", "", k) for k in both]
                     + [("hi", n, "all") for n in DIRECT] + [("hi", "soul", "all")]
                     + [("hi", "qk" + n, k) for n in "13" for k in both])
        DVE_STEPS = ([("lo", n, k) for n in TURNED for k in both] + [("lo", n, "all") for n in DIRECT]
                     + [("lo", "soul", "all")] + [("lo", "qk" + n, k) for n in "13" for k in both]
                     + [("zero", "", ""), ("scale", "q0", ""), ("scale", "q2", ""), ("scale", "soul_b", ""),
                        ("sum", "1", ""), ("neg", "1", ""), ("sum", "3", ""), ("neg", "3", ""), ("out_bias", "", "")])
        STREAM = {"0": "A", "2": "B"}
        act_step = {key: i + 1 for i, key in enumerate(ACT_STEPS)}
        dve_step = {key: i + 1 for i, key in enumerate(DVE_STEPS)}
        SETUP_DONE = len(DVE_STEPS)

        setup_fills = []
        for i, key in enumerate(["t_q0", "t_k0", "t_v0", "t_o0", "t_f1", "t_f3", "qk1", "qk3", "c1", "c3", "out_bias"]):
            n_k = KT if key[:2] in ("t_", "qk") else 1
            setup_fills += [((key, k), (2 * i + k) % BANKS) for k in range(n_k)]
        setup = Setup(setup_fills)

        LOOP_START = (LAST_LAG + 2 + 1) // 2 * 2
        LOOP_END = (GROUPS + FIRST_LAG) // 2 * 2
        LAGS = range(FIRST_LAG, LAST_LAG + 1)

        def straight(t, start, held):
            return Turn(t, t % 2, [lag for lag in LAGS if 0 <= t - lag < GROUPS], start, held)

        before, start, held = [], setup.count, {b: (("setup", "", 0), 0) for b in range(BANKS) if b not in HEADS_BANK.values()}
        for t in range(FIRST_LAG, LOOP_START):
            before.append(straight(t, start, held))
            start, held = [n + c for n, c in zip(start, before[-1].count)], before[-1].held
        loop_start, loop_held = start, held
        full = Turn(LOOP_START, 0, LAGS, start, held)
        assert full.held == held
        start = [n + c * (LOOP_END - LOOP_START) for n, c in zip(start, full.count)]
        after = []
        for t in range(LOOP_END, GROUPS + LAST_LAG):
            after.append(straight(t, start, held))
            start, held = [n + c for n, c in zip(start, after[-1].count)], after[-1].held

        def run(eng, task):
            for turn in before:
                task(turn)
            with eng.Fori(LOOP_START, LOOP_END, 2) as t:
                for odd in range(2):
                    task(Turn(t + odd, odd, LAGS,
                              [n + (t + (odd - LOOP_START)) * c for n, c in zip(loop_start, full.count)], loop_held))
            for turn in after:
                task(turn)

        def last_reader(key, t):
            name, where, n = key
            g = t - LAG[key]
            stream = STREAM.get(where)
            if name in ("scores", "turn"):
                return (exped if name == "scores" else pt_ready)[where], UNITS * g + n + 1
            if name == "v":
                return v_ready[stream], V_PARTS[stream] * g + n + 1
            if name in ("q", "k"):
                return (qt_ready if name == "q" else kt_ready)[stream], KT * (g + 1)
            if name == "fc":
                return fp_ready[where], GROUP * g + n + 1
            if name == "out_proj":
                return summed, GROUP * g + n + 1
            if name == "turn_back":
                return x3_scaled, GROUP * g + n + 1
            if name == "mask":
                return masked[where], GROUP * (g + 1)
            if name == "mix":
                return (x2_ready if where == "1" else out_ready), GROUP * (g + 1)
            return {"turn_x": xt_ready.get(where), "turn_p": fpt_ready.get(where),
                    "turn_rows": ac_rows_ready}[name], g + 1

        def wait_drained(pe, turn, *key):
            former, back = turn.before[key]
            if former[0] != "setup":
                pe.wait_ge(*last_reader(former, turn.t - back))

        def cols(n, width=P):
            return slice(n * width, (n + 1) * width)

        block = ctx.enter_context(nc.Block())

        @block.sync
        def _(sp):
            for n in RAW_ORDER:
                sp.dma_start(raw[n], ins[SOURCE[n]].rearrange("(k p) e -> p k e", p=P)).then_inc(raw_landed, 16)

            def spread(stream, G):
                sp.wait_ge(kt_ready[stream], KT * (G.no + 1))
                for h in range(HALF):
                    part = slice(h * HEAD_DIM, (h + 1) * HEAD_DIM)
                    sp.dma_start(kt_diag[stream][part, G.odd, :, :, h, :],
                                 kt[stream][part, :, :].rearrange("p k (g n) -> p k g n", g=GROUP)
                                 ).then_inc(kd_landed[stream], 16)

            def turn(turn):
                for name, where, n, G in turn.steps("sync"):
                    if name == "load":
                        G.wait_former(sp, xt_ready["0"], 1, 1)
                        G.wait_former(sp, x_biased["0"], 1, 1)
                        sp.dma_start(x_in[:, :, :], x_dram[G.no]).then_inc(x_landed, 16)
                        G.wait_former(sp, adj_m_ready, 1, 2)
                        sp.dma_start(adj[:, G.odd, :, :], adj_dram[G.no]).then_inc(adj_landed, 16)
                    elif name == "spread":
                        spread(where, G)
                    elif name == "store":
                        sp.wait_ge(out_ready, GROUP * (G.no + 1))
                        sp.dma_start(out_dram[G.no], x_out[:, :, :]).then_inc(stored, 16)

            run(sp, turn)
            sp.wait_ge(stored, 16 * GROUPS)

        @block.gpsimd
        def _(pool):
            pool.memset(ident[:, :], 0.0).then_inc(const_ready, 1)
            pool.wait_ge(const_ready, 1)
            pool.affine_select(out=ident[:, :], in_=ident[:, :], compare_op=ALU.not_equal, fill=1.0,
                               base=0, pattern=[[-1, P]], channel_multiplier=1).then_inc(const_ready, 1)
            for tile, value in ((one, 1.0), (big, PENALTY), (adj_eps, ADJ_EPS), (ln_eps, LN_EPS), (minus_half, -0.5)):
                pool.memset(tile[:, :], value).then_inc(const_ready, 1)
            pool.memset(ac_cols[:, :, :].bitcast(F32), 1.0).then_inc(const_ready, 1)
            for s in "AB":
                pool.memset(kt_diag[s][:, :, :, :, :, :], 0.0).then_inc(const_ready, 1)

            def everywhere(cell, shape=(P, GROUP, P)):
                return cell[:, :].unsqueeze(2).broadcast_to(list(shape))

            def make_penalty(layer, source, G):
                G.wait_former(pool, masked[layer], GROUP, 1)
                pool.wait_ge(adj_m_ready if source is adj_m else adj_n_ready, G.no + 1)
                pool.tensor_tensor(penalty[layer][:, :, :], everywhere(one), source[:, G.odd, :, :], ALU.subtract
                                   ).then_inc(one_minus[layer], 1)
                pool.wait_ge(one_minus[layer], G.no + 1)
                pool.tensor_tensor(penalty[layer][:, :, :], penalty[layer][:, :, :], everywhere(big), ALU.mult
                                   ).then_inc(penalty_ready[layer], 1)

            def add_row(result, x, row_tile):
                return pool.tensor_tensor(result, x, row_tile[:, :].unsqueeze(1).broadcast_to([P, GROUP, DIM]),
                                          ALU.add)

            def spread_inverse(u, G):
                g, half = divmod(u, 2)
                pool.wait_ge(inverted["A"], UNITS * G.no + u + 1)
                pool.tensor_tensor(inv_wide[:, u % 2, :].rearrange("p (h d) -> p h d", h=HALF),
                                   inv_den["A"][:, G.odd, g, half * HALF:(half + 1) * HALF].unsqueeze(2).broadcast_to(
                                       [P, HALF, HEAD_DIM]), everywhere(one, (P, HALF, HEAD_DIM)), ALU.mult
                                   ).then_inc(inv_spread, 1)

            def turn(turn):
                for name, where, n, G in turn.steps("gpsimd"):
                    if name == "bias":
                        if where == "0":
                            pool.wait_ge(x_landed, 16 * (G.no + 1))
                            G.wait_former(pool, summed, GROUP, 2)
                            pool.wait_ge(adj_landed, 16 * (G.no + 1))
                            G.wait_former(pool, weighed["A"], UNITS, 2)
                            last = add_row(x_0[:, G.odd, :, :], x_in[:, :, :], out_bias)
                        elif where == "2":
                            pool.wait_ge(x2_ready, GROUP * (G.no + 1))
                            G.wait_former(pool, x3_ready, 1, 2)
                            last = add_row(x_2b[:, G.odd, :, :], x_2[:, :, :], rows["b2"])
                        else:
                            key = ("turn_x", where, 0)
                            pool.wait_ge(filled[turn.bank(*key)], turn.after(*key))
                            x = (x_1 if where == "1" else x_3)[:, G.odd, :, :]
                            last = add_row(x, x, rows["b" + where])
                        last.then_inc(x_biased[where], 1)
                    elif name == "adj_0":
                        pool.tensor_scalar(adj_0[:, G.odd, :, :], adj[:, G.odd, :, :], ADJ_MIN, 1.0, ALU.max, ALU.mult
                                           ).then_inc(adj0_ready, 1)
                    elif name in ("adj_m", "adj_n"):
                        to, source = (adj_m, adj) if name == "adj_m" else (adj_n, adj_m)
                        if name == "adj_m":
                            pool.wait_ge(adj_landed, 16 * (G.no + 1))
                            G.wait_former(pool, adj_n_ready, 1, 2)
                        else:
                            G.wait_former(pool, penalty_ready["3"], 1, 2)
                            pool.wait_ge(adj_m_ready, G.no + 1)
                        pool.tensor_tensor(to[:, G.odd, :, :], source[:, G.odd, :, :], everywhere(one), ALU.mult
                                           ).then_inc(adj_m_ready if name == "adj_m" else adj_n_ready, 1)
                    elif name == "adj_2":
                        G.wait_former(pool, weighed["B"], UNITS, 2)
                        pool.wait_ge(adj_m_ready, G.no + 1)
                        pool.tensor_tensor(adj_2[:, G.odd, :, :], adj_m[:, G.odd, :, :], everywhere(adj_eps), ALU.add
                                           ).then_inc(adj2_ready, 1)
                    elif name == "penalty":
                        make_penalty(where, adj_m if where == "1" else adj_n, G)
                    elif name == "turn" and where == "A":
                        spread_inverse(n, G)
                    elif name == "rstd":
                        pool.wait_ge(moments_ready, GROUP * (G.no + 1))
                        pool.tensor_tensor(rstd[:, :], moments[:, :, 1], ln_eps[:, :].broadcast_to([P, GROUP]), ALU.add
                                           ).then_inc(var_ready, 1)
                        pool.wait_ge(var_ready, G.no + 1)
                        pool.tensor_tensor(rstd[:, :], rstd[:, :], minus_half[:, :].broadcast_to([P, GROUP]), ALU.pow
                                           ).then_inc(rstd_ready, 1)
                    elif name == "x_3":
                        pool.wait_ge(x_biased["2"], G.no + 1)
                        pool.wait_ge(x3_scaled, GROUP * (G.no + 1))
                        pool.tensor_tensor(x_3[:, G.odd, :, :], x_3[:, G.odd, :, :], x_2b[:, G.odd, :, :], ALU.add
                                           ).then_inc(x3_ready, 1)

            pool.wait_ge(small_landed, SMALL_DONE)
            pool.wait_ge(setup_dve, SETUP_DONE)
            pool.wait_ge(const_ready, CONSTANTS)
            run(pool, turn)

        @block.scalar
        def _(act):
            for tile, src in small:
                act.dma_start(tile, src).then_inc(small_landed, 16)
            act.wait_ge(raw_landed, 16 * len(RAW_ORDER))

            for n in TURNED:
                for k in range(KT):
                    b = setup.bank("t_" + n, k)
                    act.wait_ge(filled[b], setup.after("t_" + n, k))
                    act.activation(w_hi[n][:, k, 0:DIM], bank[b][:, 0:DIM], ACT.Copy).then_inc(setup_act, 1)
            for k in range(KT):
                b = setup.bank("t_f3", k)
                act.wait_ge(filled[b], setup.after("t_f3", k))
                act.activation(w3_t[:, k, :], bank[b][:, 0:DIM], ACT.Copy
                               ).then_inc(setup_act, 1)
            for n in DIRECT:
                act.activation(w_hi[n][:, :, 0:DIM], raw[n], ACT.Copy).then_inc(setup_act, 1)
            act.wait_ge(small_landed, SMALL_DONE)
            act.activation(w_hi["v2"][:, :, DIM:WIDE], soul_w[:, :, :], ACT.Copy, scale=-1.0).then_inc(setup_act, 1)
            for n in "13":
                for k in range(KT):
                    b = setup.bank("qk" + n, k)
                    act.wait_ge(filled[b], setup.after("qk" + n, k))
                    act.activation(w_hi["f" + n][:, k, DIM:WIDE], bank[b][:, 0:2], ACT.Copy, scale=-1.0
                                   ).then_inc(setup_act, 1)

            def turn(turn):
                for name, where, n, G in turn.steps("scalar"):
                    key = (name, where, n)
                    if key in turn.place:
                        b = turn.bank(*key)
                    if name == "weigh":
                        act.wait_ge(maxed[where], UNITS * G.no + n + 1)
                        b = SCORE_BANK[where]
                        for h in range(HALF):
                            last = act.activation(e[where][:, n % 2, cols(h)], bank[b][:, cols(h)], ACT.Exp,
                                                  bias=neg_max[where][:, n % 2, h:h + 1], scale=-1.0)
                        last.then_inc(exped[where], 1)
                    elif name == "turn":
                        act.wait_ge(filled[b], turn.after(*key))
                        act.activation(pt[where][:, n % 2, :], bank[b][:, :], ACT.Copy).then_inc(pt_ready[where], 1)
                    elif name == "finish":
                        act.wait_ge(heads_ready[where], GROUP * G.no + n + 1)
                        if where == "A":
                            act.activation(inv_den_t[:, n, :], bank[HEADS_BANK["A"]][:, DIM:2 * DIM], ACT.Copy
                                           ).then_inc(inv_t_ready, 1)
                        else:
                            act.activation(ot["B"][:, n, :], bank[HEADS_BANK["B"]][:, 0:DIM], ACT.Copy
                                           ).then_inc(ot_ready["B"], 1)
                    elif name == "split":
                        act.wait_ge(ot_ready["A"], GROUP * G.no + n + 1)
                        act.activation(ot_hi[:, n, :], ot["A"][:, n, :], ACT.Copy).then_inc(ot_hi_ready, 1)
                    elif name == "turn_x":
                        act.wait_ge(filled[b], turn.after(*key))
                        act.activation(xt_hi[where][:, :, :].rearrange("p k n -> p (k n)"), bank[b][:, :], ACT.Copy
                                       ).then_inc(xt_hi_ready[where], 1)
                    elif name == "k":
                        s = STREAM[where]
                        G.wait_former(act, kd_landed[s], 16 * HALF, 1)
                        act.wait_ge(filled[b], turn.after(*key))
                        for k in range(KT):
                            act.activation(kt[s][:, k, :], bank[b][:, cols(k, GROUP * P)], ACT.Identity,
                                           bias=bias_cols["k" + where][:, k:k + 1]).then_inc(kt_ready[s], 1)
                    elif name == "q":
                        s = STREAM[where]
                        act.wait_ge(filled[b], turn.after(*key))
                        for k in range(KT):
                            act.activation(qt[s][:, G.odd, k, :], bank[b][:, cols(k, GROUP * P)], ACT.Identity,
                                           bias=bias_cols["q" + where][:, k:k + 1], scale=-SCALE
                                           ).then_inc(qt_ready[s], 1)
                    elif name == "v":
                        act.wait_ge(filled[b], turn.after(*key))
                        if where == "0":
                            act.activation(v["A"][:, G.odd, :, :].rearrange("p g d -> p (g d)"), bank[b][:, :],
                                           ACT.Copy).then_inc(v_ready["A"], 1)
                        else:
                            act.activation(v["B"][:, G.odd, n, :], bank[b][:, 0:WIDE], ACT.Copy
                                           ).then_inc(v_ready["B"], 1)
                    elif name == "fc":
                        act.wait_ge(filled[b], turn.after(*key))
                        act.activation(fp[where][:, n, :], bank[b][:, 0:WIDE], ACT.Copy).then_inc(fp_ready[where], 1)
                    elif name == "exp":
                        act.wait_ge(f_maxed[where], G.no + 1)
                        for g in range(GROUP):
                            last = act.activation(logits[where][:, g, :], logits[where][:, g, :], ACT.Exp,
                                                  bias=f_neg_max[where][:, g:g + 1], scale=-1.0,
                                                  accum_out=f_den[where][:, g:g + 1])
                        last.then_inc(f_exped[where], 1)
                    elif name == "turn_p":
                        act.wait_ge(filled[b], turn.after(*key))
                        act.activation(fpt[where][:, :, :].rearrange("p g n -> p (g n)"), bank[b][:, 0:GROUP * P],
                                       ACT.Copy).then_inc(fpt_ready[where], 1)
                    elif name == "turn_rows":
                        act.wait_ge(filled[b], turn.after(*key))
                        act.activation(ac_rows[:, :, :].rearrange("p r n -> p (r n)"), bank[b][0:4, :], ACT.Copy
                                       ).then_inc(ac_rows_ready, 1)

            act.wait_ge(setup_dve, SETUP_DONE)
            run(act, turn)

        @block.vector
        def _(dve):
            def low_part(out_tile, src, hi_tile):
                return dve.tensor_tensor(out_tile, src, hi_tile.bitcast(F32), ALU.subtract)

            dve.wait_ge(raw_landed, 16 * len(RAW_ORDER))
            for n in TURNED:
                for k in range(KT):
                    b = setup.bank("t_" + n, k)
                    dve.wait_ge(setup_act, act_step["hi", n, k])
                    low_part(w_lo[n][:, k, 0:DIM], bank[b][:, 0:DIM], w_hi[n][:, k, 0:DIM]
                             ).then_inc(setup_dve, 1)
            for n in DIRECT:
                dve.wait_ge(setup_act, act_step["hi", n, "all"])
                low_part(w_lo[n][:, :, 0:DIM], raw[n], w_hi[n][:, :, 0:DIM]).then_inc(setup_dve, 1)
            dve.wait_ge(small_landed, SMALL_DONE)
            dve.wait_ge(setup_act, act_step["hi", "soul", "all"])
            dve.scalar_tensor_tensor(w_lo["v2"][:, :, DIM:WIDE], soul_w[:, :, :], -1.0,
                                     w_hi["v2"][:, :, DIM:WIDE].bitcast(F32), ALU.mult, ALU.subtract
                                     ).then_inc(setup_dve, 1)
            for n in "13":
                for k in range(KT):
                    b = setup.bank("qk" + n, k)
                    dve.wait_ge(setup_act, act_step["hi", "qk" + n, k])
                    dve.scalar_tensor_tensor(w_lo["f" + n][:, k, DIM:WIDE], bank[b][:, 0:2], -1.0,
                                             w_hi["f" + n][:, k, DIM:WIDE].bitcast(F32), ALU.mult, ALU.subtract
                                             ).then_inc(setup_dve, 1)
            dve.memset(soul_b[:, 1:2], 0.0).then_inc(setup_dve, 1)
            for n in ("q0", "q2"):
                dve.tensor_scalar(bias_cols[n][:, :], bias_cols[n][:, :], -SCALE, None, ALU.mult
                                  ).then_inc(setup_dve, 1)
            dve.wait_ge(setup_dve, dve_step["zero", "", ""])
            dve.tensor_scalar(soul_b[:, :], soul_b[:, :], -1.0, None, ALU.mult).then_inc(setup_dve, 1)
            for n in "13":
                b = setup.bank("c" + n, 0)
                dve.wait_ge(filled[b], setup.after("c" + n, 0))
                dve.tensor_tensor(qk_b[n][:, :], bank[b][:, 0:2], qk_b[n][:, :], ALU.add
                                  ).then_inc(setup_dve, 1)
                dve.wait_ge(setup_dve, dve_step["sum", n, ""])
                dve.tensor_scalar(qk_b[n][:, :], qk_b[n][:, :], -1.0, None, ALU.mult).then_inc(setup_dve, 1)
            b = setup.bank("out_bias", 0)
            dve.wait_ge(filled[b], setup.after("out_bias", 0))
            dve.tensor_tensor(out_bias[:, :], bank[b][:, 0:DIM], out_bias[:, :], ALU.add
                              ).then_inc(setup_dve, 1)

            def mask(layer, G, turn):
                key = ("mask", layer, 0)
                b = turn.bank(*key)
                dve.wait_ge(penalty_ready[layer], G.no + 1)
                dve.wait_ge(filled[b], turn.after(*key))
                for g in range(GROUP):
                    dve.scalar_tensor_tensor(logits[layer][:, g, :], bank[b][:, cols(g)],
                                             fp[layer][:, g, DIM:DIM + 1], penalty[layer][:, g, :],
                                             ALU.add, ALU.add).then_inc(masked[layer], 1)
                dve.wait_ge(masked[layer], GROUP * (G.no + 1))
                dve.scalar_tensor_tensor(logits[layer][:, :, :], logits[layer][:, :, :], SLOPE,
                                         logits[layer][:, :, :], ALU.mult, ALU.min).then_inc(leaked[layer], 1)
                dve.wait_ge(leaked[layer], G.no + 1)
                dve.tensor_reduce(f_neg_max[layer][:, :], logits[layer][:, :, :], axis=AX.X, op=ALU.min
                                  ).then_inc(f_maxed[layer], 1)

            def residual(layer, G, turn):
                result, ready, x = (x_2, x2_ready, x_1) if layer == "1" else (x_out, out_ready, x_3)
                dve.wait_ge(f_exped[layer], G.no + 1)
                dve.reciprocal(f_inv[layer][:, :], f_den[layer][:, :]).then_inc(f_inverted[layer], 1)
                dve.wait_ge(x_biased[layer], G.no + 1)
                if layer == "1":
                    G.wait_former(dve, x_biased["2"], 1, 1)
                else:
                    G.wait_former(dve, stored, 16, 1)
                dve.wait_ge(f_inverted[layer], G.no + 1)
                b = turn.bank("mix", layer, 0)
                dve.wait_ge(filled[b], turn.after("mix", layer, 0))
                for g in range(GROUP):
                    dve.scalar_tensor_tensor(result[:, g, :], bank[b][:, cols(g, DIM)], f_inv[layer][:, g:g + 1],
                                             x[:, G.odd, g, :], ALU.mult, ALU.add).then_inc(ready, 1)

            def centre(g, G):
                x = x_1[:, G.odd, g, :]
                dve.scalar_tensor_tensor(x, x, moments[:, g, 0:1], rows["gamma"][:, :], ALU.subtract, ALU.mult
                                         ).then_inc(centred, 1)

            def turn(turn):
                for name, where, n, G in turn.steps("vector"):
                    key = (name, where, n)
                    if key in turn.place:
                        b = turn.bank(*key)
                    if name == "scores":
                        dve.wait_ge(filled[b], turn.after(*key))
                        dve.tensor_reduce(neg_max[where][:, n % 2, :], bank[b][:, :].rearrange("p (h n) -> p h n", h=HALF),
                                          axis=AX.X, op=ALU.min).then_inc(maxed[where], 1)
                    elif name == "weigh":
                        if n == 0:
                            dve.wait_ge(adj0_ready if where == "A" else adj2_ready, G.no + 1)
                        dve.wait_ge(exped[where], UNITS * G.no + n + 1)
                        for h in range(HALF):
                            last = dve.tensor_tensor_reduce(
                                out=pr[where][:, n % 2, cols(h)], in0=e[where][:, n % 2, cols(h)],
                                in1=weight_of[where][:, G.odd, n // 2, :], scale=1.0, scalar=0.0,
                                op0=ALU.mult, op1=ALU.add, accum_out=den[where][:, n % 2, h:h + 1])
                        last.then_inc(weighed[where], 1)
                    elif name == "turn":
                        g, half = divmod(n, 2)
                        dve.wait_ge(weighed[where], UNITS * G.no + n + 1)
                        dve.reciprocal(inv_den[where][:, G.odd, g, half * HALF:(half + 1) * HALF],
                                       den[where][:, n % 2, :]).then_inc(inverted[where], 1)
                    elif name == "finish" and where == "A":
                        dve.wait_ge(inv_t_ready, GROUP * G.no + n + 1)
                        dve.tensor_tensor(ot["A"][:, n, :], bank[HEADS_BANK["A"]][:, 0:DIM], inv_den_t[:, n, :],
                                          ALU.mult).then_inc(ot_ready["A"], 1)
                    elif name == "split":
                        dve.wait_ge(ot_hi_ready, GROUP * G.no + n + 1)
                        low_part(ot_lo[:, n, :], ot["A"][:, n, :], ot_hi[:, n, :]).then_inc(ot_lo_ready, 1)
                    elif name == "out_proj":
                        if n == 0:
                            dve.wait_ge(x_biased["0"], G.no + 1)
                        else:
                            dve.wait_ge(stats_ready, GROUP * G.no + n)
                        dve.wait_ge(filled[b], turn.after(*key))
                        dve.tensor_tensor(x_1[:, G.odd, n, :], bank[b][:, 0:DIM], x_0[:, G.odd, n, :], ALU.add
                                          ).then_inc(summed, 1)
                        dve.wait_ge(summed, GROUP * G.no + n + 1)
                        dve.bn_stats(stats[:, n, :], x_1[:, G.odd, n, :]).then_inc(stats_ready, 1)
                        if n > 0:
                            dve.bn_aggr(moments[:, n - 1, :], stats[:, n - 1, :]).then_inc(moments_ready, 1)
                        if n == GROUP - 1:
                            dve.wait_ge(moments_ready, GROUP * G.no + n)
                            dve.wait_ge(stats_ready, GROUP * (G.no + 1))
                            for g in range(n):
                                centre(g, G)
                            dve.bn_aggr(moments[:, n, :], stats[:, n, :]).then_inc(moments_ready, 1)
                    elif name == "norm":
                        dve.wait_ge(moments_ready, GROUP * (G.no + 1))
                        centre(GROUP - 1, G)
                        dve.wait_ge(rstd_ready, G.no + 1)
                        for g in range(GROUP):
                            dve.wait_ge(centred, GROUP * G.no + g + 1)
                            x = x_1[:, G.odd, g, :]
                            dve.scalar_tensor_tensor(x, x, rstd[:, g:g + 1], rows["beta"][:, :], ALU.mult, ALU.add
                                                     ).then_inc(x1_ready, 1)
                    elif name == "turn_back":
                        if n == 0:
                            dve.wait_ge(inverted["B"], UNITS * G.no + 2)
                        else:
                            dve.wait_ge(inverted["B"], UNITS * G.no + 2 * (n + 1))
                        dve.wait_ge(filled[b], turn.after(*key))
                        dve.tensor_tensor(
                            x_3[:, G.odd, n, :].rearrange("p (h d) -> p h d", h=HEADS),
                            bank[b][:, 0:DIM].rearrange("p (h d) -> p h d", h=HEADS),
                            inv_den["B"][:, G.odd, n, :].unsqueeze(2).broadcast_to([P, HEADS, HEAD_DIM]), ALU.mult
                        ).then_inc(x3_scaled, 1)
                    elif name == "turn_x":
                        dve.wait_ge(xt_hi_ready[where], G.no + 1)
                        low_part(xt_lo[where][:, :, :].rearrange("p k n -> p (k n)"), bank[b][:, :],
                                 xt_hi[where][:, :, :].rearrange("p k n -> p (k n)")).then_inc(xt_ready[where], 1)
                    elif name == "qk":
                        dve.wait_ge(fp_ready[where], GROUP * (G.no + 1))
                        qk = fp[where][:, :, DIM:WIDE]
                        dve.tensor_tensor(qk, qk, qk_b[where][:, :].unsqueeze(1).broadcast_to([P, GROUP, 2]), ALU.add
                                          ).then_inc(qk_ready[where], 1)
                    elif name == "mask":
                        mask(where, G, turn)
                    elif name == "mix":
                        residual(where, G, turn)
                    elif name == "ac":
                        dve.wait_ge(v_ready["B"], GROUP * (G.no + 1))
                        dve.tensor_tensor(ac_sum[:, :, :], v["B"][:, G.odd, :, DIM:WIDE],
                                          soul_b[:, :].unsqueeze(1).broadcast_to([P, GROUP, 2]), ALU.add
                                          ).then_inc(ac_summed, 1)
                        dve.wait_ge(ac_summed, G.no + 1)
                        dve.tensor_copy(ac_cols[:, :, 0:7:6], ac_sum[:, :, :]).then_inc(ac_hi_ready, 1)
                        dve.wait_ge(ac_hi_ready, G.no + 1)
                        low_part(ac_cols[:, :, 1:8:6], ac_sum[:, :, :], ac_cols[:, :, 0:7:6]).then_inc(ac_ready, 1)

            dve.wait_ge(setup_dve, SETUP_DONE)
            dve.wait_ge(const_ready, CONSTANTS)
            run(dve, turn)

        @block.tensor
        def _(pe):
            def three_pass(out_ap, left_hi, left_lo, right_hi, right_lo):
                for k in range(KT):
                    pe.matmul(out_ap, left_hi(k), right_hi(k), start=(k == 0), stop=False)
                    pe.matmul(out_ap, left_lo(k), right_hi(k), start=False, stop=False)
                    last = pe.matmul(out_ap, left_hi(k), right_lo(k), start=False, stop=(k == KT - 1))
                return last

            def drained_setup(*key):
                if setup.before[key] is not None:
                    name, k = setup.before[key]
                    if name == "t_f3":
                        pe.wait_ge(setup_act, act_step["w3_t", "", k])
                    else:
                        pe.wait_ge(setup_dve, dve_step["lo", name[2:] if name[:2] == "t_" else name, k])

            pe.wait_ge(raw_landed, 16 * len(RAW_ORDER))
            pe.wait_ge(const_ready, 2)
            for n in TURNED + ("f3",):
                for k in range(KT):
                    b = setup.bank("t_" + n, k)
                    drained_setup("t_" + n, k)
                    for j in range(KT):
                        last = pe.transpose(bank[b][:, cols(j)], raw[n][:, j, cols(k)], ident[:, :])
                    last.then_inc(filled[b], 1)
            pe.wait_ge(small_landed, SMALL_DONE)
            for n in "13":
                if n == "3":
                    pe.wait_ge(setup_act, act_step["w3_t", "", KT - 1])
                by_row = raw["f1"] if n == "1" else w3_t
                for k in range(KT):
                    b = setup.bank("qk" + n, k)
                    drained_setup("qk" + n, k)
                    for j in range(KT):
                        last = pe.matmul(bank[b][:, 0:2], by_row[:, j, cols(k)], qk_w[n][:, j, :],
                                         start=(j == 0), stop=(j == KT - 1))
                    last.then_inc(filled[b], 1)
            for n in "13":
                b = setup.bank("c" + n, 0)
                drained_setup("c" + n, 0)
                for j in range(KT):
                    last = pe.matmul(bank[b][:, 0:2], fc_bias_col[n][:, j:j + 1].broadcast_to([P, P]),
                                     qk_w[n][:, j, :], start=(j == 0), stop=(j == KT - 1))
                last.then_inc(filled[b], 1)
            b = setup.bank("out_bias", 0)
            drained_setup("out_bias", 0)
            pe.wait_ge(setup_dve, dve_step["lo", "o0", KT - 1])
            for j in range(KT):
                for part in (w_hi, w_lo):
                    last = pe.matmul(bank[b][:, 0:DIM], bv_col[:, j:j + 1].broadcast_to([P, P]),
                                     part["o0"][:, j, 0:DIM].bitcast(F32), start=(j == 0 and part is w_hi),
                                     stop=(j == KT - 1 and part is w_lo))
            last.then_inc(filled[b], 1)

            def scores(s, u, G, turn):
                g, half = divmod(u, 2)
                b = turn.bank("scores", s, u)
                if u == 0:
                    pe.wait_ge(qt_ready[s], KT * (G.no + 1))
                    pe.wait_ge(kd_landed[s], 16 * HALF * (G.no + 1))
                    if s == "B":
                        pe.wait_ge(ac_rows_ready, G.no + 1)
                wait_drained(pe, turn, "scores", s, u)
                last = pe.matmul(bank[b][:, :], qt[s][:, G.odd, half, cols(g)], kt_diag[s][:, G.odd, half, g, :, :],
                                 start=True, stop=(s == "A"))
                if s == "B":
                    last = pe.matmul(bank[b][:, :], ac_rows[:, 0, cols(g)],
                                     ac_rows[:, 1, cols(g)].unsqueeze(1).broadcast_to([4, HALF, P]),
                                     start=False, stop=True)
                last.then_inc(filled[b], 1)

            def turn_probabilities(s, u, G, turn):
                b = turn.bank("turn", s, u)
                pe.wait_ge(weighed[s], UNITS * G.no + u + 1)
                wait_drained(pe, turn, "turn", s, u)
                for h in range(HALF):
                    last = pe.transpose(bank[b][:, cols(h)], pr[s][:, u % 2, cols(h)], ident[:, :])
                last.then_inc(filled[b], 1)

            def use(s, u, G):
                g, half = divmod(u, 2)
                b = HEADS_BANK[s]
                if half == 0:
                    read = GROUP * G.no + g
                    if not isinstance(read, int) or read > 0:
                        pe.wait_ge(ot_ready[s], read)
                if u == 0:
                    pe.wait_ge(v_ready[s], V_PARTS[s] * (G.no + 1))
                pe.wait_ge(pt_ready[s], UNITS * G.no + u + 1)
                for h in range(HALF):
                    head = (half * HALF + h) * HEAD_DIM
                    part = slice(h * HEAD_DIM, (h + 1) * HEAD_DIM)
                    last = pe.matmul(bank[b][part, cols(half)], v[s][:, G.odd, g, head:head + HEAD_DIM],
                                     pt[s][:, u % 2, cols(h)], start=True, stop=True)
                if s == "A":
                    pe.wait_ge(inv_spread, UNITS * G.no + u + 1)
                    last = pe.transpose(bank[b][:, cols(2 + half)], inv_wide[:, u % 2, :], ident[:, :])
                if half == 1:
                    last.then_inc(heads_ready[s], 1)

            def turn(turn):
                for name, where, n, G in turn.steps("tensor"):
                    key = (name, where, n)
                    if name == "scores":
                        scores(where, n, G, turn)
                    elif name == "turn":
                        turn_probabilities(where, n, G, turn)
                    elif name == "use":
                        use(where, n, G)
                    elif key in turn.place:
                        wait_drained(pe, turn, *key)
                        b = turn.bank(*key)
                        other(name, where, n, G, bank[b]).then_inc(filled[b], 1)

            X = {"0": (x_in, x_landed, 16), "1": (x_1, x1_ready, GROUP), "2": (x_2, x2_ready, GROUP),
                 "3": (x_3, x3_ready, 1)}

            def other(name, layer, n, G, to):
                if name == "turn_x":
                    x, ready, per_group = X[layer]
                    pe.wait_ge(ready, per_group * (G.no + 1))
                    for k in range(KT):
                        for g in range(GROUP):
                            last = pe.transpose(to[:, cols(k * GROUP + g)],
                                                (x[:, g, cols(k)] if layer in "02" else x[:, G.odd, g, cols(k)]),
                                                ident[:, :])
                    return last
                if name in ("q", "k"):
                    pe.wait_ge(xt_ready[layer], G.no + 1)
                    w = name + layer
                    for m in range(KT):
                        last = three_pass(to[:, cols(m, GROUP * P)],
                                          lambda k: w_hi[w][:, k, cols(m)], lambda k: w_lo[w][:, k, cols(m)],
                                          lambda k: xt_hi[layer][:, k, :], lambda k: xt_lo[layer][:, k, :])
                    return last
                if name in ("v", "fc"):
                    pe.wait_ge(xt_ready[layer], G.no + 1)
                    w = name[0] + layer
                    width = DIM if layer == "0" else WIDE
                    for i, g in enumerate(range(GROUP) if layer == "0" else [n]):
                        last = three_pass(to[:, i * DIM:i * DIM + width],
                                          lambda k: xt_hi[layer][:, k, cols(g)], lambda k: xt_lo[layer][:, k, cols(g)],
                                          lambda k: w_hi[w][:, k, 0:width], lambda k: w_lo[w][:, k, 0:width])
                    return last
                if name == "out_proj":
                    pe.wait_ge(ot_lo_ready, GROUP * G.no + n + 1)
                    return three_pass(to[:, 0:DIM],
                                      lambda k: ot_hi[:, n, cols(k)], lambda k: ot_lo[:, n, cols(k)],
                                      lambda k: w_hi["o0"][:, k, 0:DIM], lambda k: w_lo["o0"][:, k, 0:DIM])
                if name == "turn_back":
                    pe.wait_ge(ot_ready["B"], GROUP * G.no + n + 1)
                    for k in range(KT):
                        last = pe.transpose(to[:, cols(k)], ot["B"][:, n, cols(k)], ident[:, :])
                    return last
                if name == "mask":
                    pe.wait_ge(qk_ready[layer], G.no + 1)
                    for g in range(GROUP):
                        last = pe.transpose(to[:, cols(g)], fp[layer][:, g, DIM + 1:WIDE].broadcast_to([P, P]),
                                            ident[:, :])
                    return last
                if name == "turn_p":
                    pe.wait_ge(f_exped[layer], G.no + 1)
                    for g in range(GROUP):
                        last = pe.transpose(to[:, cols(g)], logits[layer][:, g, :], ident[:, :])
                    return last
                if name == "mix":
                    pe.wait_ge(fpt_ready[layer], G.no + 1)
                    for g in range(GROUP):
                        last = pe.matmul(to[:, cols(g, DIM)], fpt[layer][:, g, :], fp[layer][:, g, 0:DIM],
                                         start=True, stop=True)
                    return last
                assert name == "turn_rows"
                pe.wait_ge(ac_ready, G.no + 1)
                for side in range(2):
                    for g in range(GROUP):
                        last = pe.transpose(to[0:4, cols(side * GROUP + g)],
                                            ac_cols[:, g, 4 * side:4 * side + 4].bitcast(F32), ident[:, :])
                return last

            pe.wait_ge(setup_dve, SETUP_DONE)
            pe.wait_ge(const_ready, CONSTANTS)
            run(pe, turn)


INPUTS = ["x", "adj", "L0_gnn_Wq", "L0_gnn_bq", "L0_gnn_Wk", "L0_gnn_bk", "L0_gnn_Wv", "L0_gnn_bv", "L0_gnn_Wo",
          "L0_gnn_bo", "L0_gnn_gamma", "L0_gnn_beta", "L1_gnn_fc_w", "L1_gnn_fc_b", "L1_gnn_q_w", "L1_gnn_q_b",
          "L1_gnn_k_w", "L1_gnn_k_b", "L2_gnn_W_q", "L2_gnn_b_q", "L2_gnn_W_k", "L2_gnn_b_k", "L2_gnn_W_v",
          "L2_gnn_b_v", "L2_gnn_w_g", "L2_gnn_b_g", "L3_gnn_W_fc", "L3_gnn_b_fc", "L3_gnn_w_q", "L3_gnn_b_q",
          "L3_gnn_w_k", "L3_gnn_b_k"]


def kernel(**inputs):
    import numpy as np
    import concourse.bacc as bacc
    from concourse.bass_utils import run_bass_kernel_spmd

    nc = bacc.Bacc("TRN2", target_bir_lowering=False, num_devices=1)
    arrays, ins = {}, {}
    for name in INPUTS:
        a = np.ascontiguousarray(inputs[name])
        if name == "L2_gnn_b_g":
            a = a.reshape(1)
        arrays[name + "_dram"] = a
        ins[name] = nc.dram_tensor(name + "_dram", a.shape, mybir.dt.from_np(a.dtype), kind="ExternalInput").ap()
    out = nc.dram_tensor("out_dram", arrays["x_dram"].shape, F32, kind="ExternalOutput").ap()
    build_kernel(nc, ins, out)
    result = run_bass_kernel_spmd(nc, [arrays], core_ids=[0])
    return result.results[0]["out_dram"]
```
